# Optimizing a Trainium2 kernel written in Bass

```python
import numpy as np
import jax
import jax.numpy as jnp

def _softmax(x, axis=-1):
    return jax.nn.softmax(x, axis=axis)

def _gelu(x):
    return jax.nn.gelu(x, approximate=True)

def _silu(x):
    return jax.nn.silu(x)

def _sigmoid(x):
    return jax.nn.sigmoid(x)

def _layernorm(x, axis=-1, eps=1e-05):
    m = jnp.mean(x, axis=axis, keepdims=True)
    v = jnp.var(x, axis=axis, keepdims=True)
    return (x - m) / jnp.sqrt(v + eps)

def _scatter_add(tgt, idx, src, axis=0):
    return tgt.at[idx].add(src)

def _segment_sum(src, seg, n):
    return jax.ops.segment_sum(src, seg, n)
kernel_name = 'mk_adaln_d4_jaxref_r8_522ac5'

def setup_inputs(seed: int=0):
    np.random.seed(seed)
    _w = jnp.asarray

    def _L0_attn_setup():
        import jax, jax.numpy as jnp
        import numpy as np
        from functools import partial
        DIM, D_STATE, D_CONV, EXPAND = (128, 16, 4, 2)
        D_INNER = DIM * EXPAND
        DT_RANK = max(1, D_INNER // 16)
        B_SZ, L = (4, 256)

        def _mamba_fwd(x, W_in, b_in, conv_k, conv_b, A_log, W_xp, b_xp, W_dt, b_dt, D_ssm, W_out, b_out):
            xz = x @ W_in + b_in
            x_proj, z = jnp.split(xz, 2, axis=-1)
            x_conv = jax.lax.conv_general_dilated(x_proj, conv_k, window_strides=(1,), padding=[(D_CONV - 1, 0)], dimension_numbers=('NWC', 'WIO', 'NWC'), feature_group_count=D_INNER) + conv_b
            xa = jax.nn.silu(x_conv)
            dtBC = xa @ W_xp + b_xp
            dt_int, B_c, C_c = jnp.split(dtBC, [DT_RANK, DT_RANK + D_STATE], axis=-1)
            dt = jax.nn.softplus(dt_int @ W_dt + b_dt)
            A = -jnp.exp(A_log)

            def step(h, inp):
                x_t, dt_t, B_t, C_t = inp
                A_bar = jnp.exp(dt_t[..., None] * A)
                h = A_bar * h + dt_t[..., None] * B_t[:, None, :] * x_t[..., None]
                y_t = jnp.sum(C_t[:, None, :] * h, axis=-1)
                return (h, y_t)
            h0 = jnp.zeros((x.shape[0], D_INNER, D_STATE), x.dtype)
            tm = lambda a: jnp.swapaxes(a, 0, 1)
            _, y = jax.lax.scan(step, h0, (tm(xa), tm(dt), tm(B_c), tm(C_c)))
            y = jnp.swapaxes(y, 0, 1) + xa * D_ssm
            return y * jax.nn.silu(z) @ W_out + b_out
        key = jax.random.key(seed)
        ks = jax.random.split(key, 12)
        s = lambda fan_in: 1.0 / np.sqrt(fan_in)
        return {'x': jax.random.normal(ks[0], (B_SZ, L, DIM), jnp.float32), 'W_in': jax.random.normal(ks[1], (DIM, 2 * D_INNER), jnp.float32) * s(DIM), 'b_in': jnp.zeros((2 * D_INNER,), jnp.float32), 'conv_k': jax.random.normal(ks[2], (D_CONV, 1, D_INNER), jnp.float32) * 0.3, 'conv_b': jnp.zeros((D_INNER,), jnp.float32), 'A_log': jax.random.normal(ks[3], (D_INNER, D_STATE), jnp.float32) * 0.02, 'W_xp': jax.random.normal(ks[4], (D_INNER, DT_RANK + 2 * D_STATE), jnp.float32) * s(D_INNER), 'b_xp': jnp.zeros((DT_RANK + 2 * D_STATE,), jnp.float32), 'W_dt': jax.random.normal(ks[5], (DT_RANK, D_INNER), jnp.float32) * s(DT_RANK), 'b_dt': jax.random.normal(ks[6], (D_INNER,), jnp.float32) * 0.02, 'D_ssm': jnp.ones((D_INNER,), jnp.float32), 'W_out': jax.random.normal(ks[7], (D_INNER, DIM), jnp.float32) * s(D_INNER), 'b_out': jnp.zeros((DIM,), jnp.float32)}
    _L0_attn_in = _L0_attn_setup()

    def _L0_ffn_setup():
        import jax, jax.numpy as jnp
        import numpy as np
        BLOCK = 16
        _GRID = jnp.array([0.0, 0.5, 1.0, 1.5, 2.0, 3.0, 4.0, 6.0], dtype=jnp.float32)
        _MID = jnp.array([0.25, 0.75, 1.25, 1.75, 2.5, 3.5, 5.0], dtype=jnp.float32)

        def fp4_quant_dequant(x):
            shape = x.shape
            xb = x.reshape(shape[:-1] + (shape[-1] // BLOCK, BLOCK))
            scale = jnp.max(jnp.abs(xb), axis=-1, keepdims=True) / 6.0
            scale = jnp.maximum(scale, jnp.float32(1e-12))
            xn = xb / scale
            idx = jnp.searchsorted(_MID, jnp.abs(xn))
            q = _GRID[idx] * jnp.sign(xn) * scale
            return q.reshape(shape)

        def fp4_linear(x, w):
            xq = fp4_quant_dequant(x)
            wq = fp4_quant_dequant(w)
            return jnp.einsum('bsk,nk->bsn', xq, wq)
        key = jax.random.key(seed)
        k1, k2, k3, k4 = jax.random.split(key, 4)
        H, I = (128, 352)
        x = jax.random.normal(k1, (4, 512, H), dtype=jnp.float32)
        w_gate = jax.random.normal(k2, (I, H), dtype=jnp.float32) * 0.02
        w_up = jax.random.normal(k3, (I, H), dtype=jnp.float32) * 0.02
        w_down = jax.random.normal(k4, (H, I), dtype=jnp.float32) * 0.02
        return {'x': x, 'w_gate': w_gate, 'w_up': w_up, 'w_down': w_down}
    _L0_ffn_in = _L0_ffn_setup()
    _L0_c = _w((lambda *s: np.random.randn(*s).astype(np.float32) * 0.05)(16, 128))
    _L0_wmod = _w((lambda *s: np.random.randn(*s).astype(np.float32) * 0.05)(128, 6 * 128) * 128 ** (-0.5))

    def _L1_attn_setup():
        import jax, jax.numpy as jnp
        import numpy as np
        B, S, D, H = (2, 256, 128, 16)
        DH = D // H
        EPS = 1e-05
        LAMBDA_INIT = 0.8
        key = jax.random.key(seed)
        ks = jax.random.split(key, 16)
        w_std = 1.0 / np.sqrt(D)
        lam_std = LAMBDA_INIT / np.sqrt(DH)
        return {'x': jax.random.normal(ks[0], (B, S, D), jnp.float32), 'Wq': jax.random.normal(ks[1], (D, D), jnp.float32) * w_std, 'bq': jax.random.normal(ks[2], (D,), jnp.float32) * 0.02, 'Wk': jax.random.normal(ks[3], (D, D), jnp.float32) * w_std, 'bk': jax.random.normal(ks[4], (D,), jnp.float32) * 0.02, 'Wv': jax.random.normal(ks[5], (D, D), jnp.float32) * w_std, 'bv': jax.random.normal(ks[6], (D,), jnp.float32) * 0.02, 'Wo': jax.random.normal(ks[7], (D, D), jnp.float32) * w_std, 'bo': jax.random.normal(ks[8], (D,), jnp.float32) * 0.02, 'lq1': jax.random.normal(ks[9], (H, DH), jnp.float32) * lam_std, 'lk1': jax.random.normal(ks[10], (H, DH), jnp.float32) * lam_std, 'lq2': jax.random.normal(ks[11], (H, DH), jnp.float32) * lam_std, 'lk2': jax.random.normal(ks[12], (H, DH), jnp.float32) * lam_std, 'gn_w': jnp.ones((H, DH), jnp.float32), 'gn_b': jnp.zeros((H, DH), jnp.float32)}
    _L1_attn_in = _L1_attn_setup()

    def _L1_ffn_setup():
        import jax, jax.numpy as jnp
        import numpy as np
        DIM = 128
        DEPTH = 6
        HEADS = 16
        DIM_HEAD = 64
        WINDOW = 32
        INNER = HEADS * DIM_HEAD
        DIM_INNER = int(DIM * 4 * 2 / 3)
        QK_SCALE = 8.0

        def shift_tokens(t):
            a, s = jnp.split(t, 2, -1)
            s = jnp.pad(s, ((0, 0), (1, 0), (0, 0)))[:, :-1]
            return jnp.concatenate([a, s], -1)

        def l2norm(t):
            return t / jnp.maximum(jnp.linalg.norm(t, axis=-1, keepdims=True), 1e-12)

        def rotate_half(x):
            x1, x2 = jnp.split(x, 2, -1)
            return jnp.concatenate([-x2, x1], -1)

        def rotary_tables(n):
            half = jnp.arange(0, DIM_HEAD, 2, dtype=jnp.float32)
            inv_freq = 1.0 / 10000.0 ** (half / DIM_HEAD)
            t = jnp.arange(n, dtype=jnp.float32)
            freqs = t[:, None] * inv_freq[None, :]
            freqs = jnp.concatenate([freqs, freqs], -1)
            base_scale = (half + 0.4 * DIM_HEAD) / (1.4 * DIM_HEAD)
            power = (t - n // 2) / (WINDOW // 2)
            scale = base_scale[None, :] ** power[:, None]
            scale = jnp.concatenate([scale, scale], -1)
            return (freqs, scale)

        def local_attention(q, k, v):
            b, h, n, d = q.shape
            w = WINDOW
            nw = n // w
            bq = q.reshape(b, h, nw, w, d)
            bk = k.reshape(b, h, nw, w, d)
            bv = v.reshape(b, h, nw, w, d)

            def look(t):
                p = jnp.pad(t, ((0, 0), (0, 0), (1, 0), (0, 0), (0, 0)))
                return jnp.concatenate([p[:, :, :nw], p[:, :, 1:]], axis=3)
            bk2, bv2 = (look(bk), look(bv))
            seq = jnp.arange(n).reshape(nw, w)
            seq_p = jnp.pad(seq, ((1, 0), (0, 0)), constant_values=-1)
            jt = jnp.concatenate([seq_p[:nw], seq_p[1:]], axis=1)
            it = seq[:, :, None]
            jb = jt[:, None, :]
            mask = (it < jb) | (it > jb + w) | (jb == -1)
            sim = jnp.einsum('bhwie,bhwje->bhwij', bq, bk2) * QK_SCALE
            sim = jnp.where(mask, -jnp.finfo(sim.dtype).max, sim)
            attn = jax.nn.softmax(sim, -1)
            out = jnp.einsum('bhwij,bhwje->bhwie', attn, bv2)
            return out.reshape(b, h, n, d)

        def attn_layer(x, Wqkv, qs, ksc, Wo):
            b, n, _ = x.shape
            qkv = x @ Wqkv
            q, k, v = jnp.split(qkv, 3, -1)
            sh = lambda t: t.reshape(b, n, HEADS, DIM_HEAD).transpose(0, 2, 1, 3)
            q, k, v = (sh(q), sh(k), sh(v))
            q = l2norm(q) * qs
            k = l2norm(k) * ksc
            freqs, scale = rotary_tables(n)
            cos, sin = (jnp.cos(freqs), jnp.sin(freqs))
            q = q * cos * scale + rotate_half(q) * sin * scale
            inv = 1.0 / scale
            k = k * cos * inv + rotate_half(k) * sin * inv
            out = local_attention(q, k, v)
            out = out.transpose(0, 2, 1, 3).reshape(b, n, INNER)
            return out @ Wo

        def ffn_layer(x, g, bln, W1, b1, W2, b2):
            mu = x.mean(-1, keepdims=True)
            var = ((x - mu) ** 2).mean(-1, keepdims=True)
            xn = (x - mu) / jnp.sqrt(var + 1e-05) * g + bln
            hg = xn @ W1 + b1
            a, gate = jnp.split(hg, 2, -1)
            return a * jax.nn.gelu(gate, approximate=False) @ W2 + b2
        key = jax.random.key(seed)
        ks = jax.random.split(key, 8)
        B, N = (2, 256)
        init = lambda k, shape: jax.random.normal(k, shape, jnp.float32) * 0.02
        return {'x': jax.random.normal(ks[0], (B, N, DIM), jnp.float32), 'Wqkv': init(ks[1], (DEPTH, DIM, 3 * INNER)), 'q_scale': jnp.ones((DEPTH, DIM_HEAD), jnp.float32), 'k_scale': jnp.ones((DEPTH, DIM_HEAD), jnp.float32), 'Wo': init(ks[2], (DEPTH, INNER, DIM)), 'ln_g': jnp.ones((DEPTH, DIM), jnp.float32), 'ln_b': jnp.zeros((DEPTH, DIM), jnp.float32), 'W1': init(ks[3], (DEPTH, DIM, 2 * DIM_INNER)), 'b1': jnp.zeros((DEPTH, 2 * DIM_INNER), jnp.float32), 'W2': init(ks[4], (DEPTH, DIM_INNER, DIM)), 'b2': jnp.zeros((DEPTH, DIM), jnp.float32)}
    _L1_ffn_in = _L1_ffn_setup()
    _L1_c = _w((lambda *s: np.random.randn(*s).astype(np.float32) * 0.05)(16, 128))
    _L1_wmod = _w((lambda *s: np.random.randn(*s).astype(np.float32) * 0.05)(128, 6 * 128) * 128 ** (-0.5))

    def _L2_attn_setup():
        import jax, jax.numpy as jnp
        import numpy as np
        D_MODEL = 128
        N_HEADS = 16
        N_GROUPS = 4
        D_HEAD = D_MODEL // N_HEADS
        HPG = N_HEADS // N_GROUPS
        B, T = (2, 256)

        def _rope(x):
            t, d = (x.shape[2], x.shape[3])
            pos = jnp.arange(t, dtype=jnp.float32)[:, None]
            freq = jnp.exp(-(jnp.arange(0, d, 2, dtype=jnp.float32) / d) * jnp.log(jnp.float32(10000.0)))
            angle = pos * freq
            cos, sin = (jnp.cos(angle), jnp.sin(angle))
            xe, xo = (x[..., ::2], x[..., 1::2])
            re = xe * cos - xo * sin
            ro = xe * sin + xo * cos
            return jnp.stack([re, ro], axis=-1).reshape(x.shape)
        key = jax.random.key(seed)
        ks = jax.random.split(key, 10)
        s = 0.02
        return {'x': jax.random.normal(ks[0], (B, T, D_MODEL), dtype=jnp.float32), 'Wq': jax.random.normal(ks[1], (D_MODEL, D_MODEL), dtype=jnp.float32) * s, 'bq': jax.random.normal(ks[2], (D_MODEL,), dtype=jnp.float32) * s, 'Wk': jax.random.normal(ks[3], (D_MODEL, N_GROUPS * D_HEAD), dtype=jnp.float32) * s, 'bk': jax.random.normal(ks[4], (N_GROUPS * D_HEAD,), dtype=jnp.float32) * s, 'Wv': jax.random.normal(ks[5], (D_MODEL, N_GROUPS * D_HEAD), dtype=jnp.float32) * s, 'bv': jax.random.normal(ks[6], (N_GROUPS * D_HEAD,), dtype=jnp.float32) * s, 'Wo': jax.random.normal(ks[7], (D_MODEL, D_MODEL), dtype=jnp.float32) * s, 'bo': jax.random.normal(ks[8], (D_MODEL,), dtype=jnp.float32) * s}
    _L2_attn_in = _L2_attn_setup()

    def _L2_ffn_setup():
        import jax, jax.numpy as jnp
        import numpy as np
        BEST_K = 2

        def _expert(xf, w1, w3, w2):
            return jax.nn.silu(xf @ w1) * (xf @ w3) @ w2
        key = jax.random.key(seed)
        ks = jax.random.split(key, 9)
        E, S_sh, D, H = (8, 2, 128, 64)
        B, S = (2, 256)
        w = lambda k, shape: jax.random.normal(k, shape, dtype=jnp.float32) * 0.02
        return {'x': jax.random.normal(ks[0], (B, S, D), dtype=jnp.float32), 'router_w': w(ks[1], (D, E)), 'router_b': jnp.zeros((E,), dtype=jnp.float32), 'routed_w1': w(ks[2], (E, D, H)), 'routed_w3': w(ks[3], (E, D, H)), 'routed_w2': w(ks[4], (E, H, D)), 'shared_w1': w(ks[5], (S_sh, D, H)), 'shared_w3': w(ks[6], (S_sh, D, H)), 'shared_w2': w(ks[7], (S_sh, H, D))}
    _L2_ffn_in = _L2_ffn_setup()
    _L2_c = _w((lambda *s: np.random.randn(*s).astype(np.float32) * 0.05)(16, 128))
    _L2_wmod = _w((lambda *s: np.random.randn(*s).astype(np.float32) * 0.05)(128, 6 * 128) * 128 ** (-0.5))

    def _L3_attn_setup():
        import jax, jax.numpy as jnp
        import numpy as np
        D_ATT_IN = 128
        NUM_HEADS = 16
        D_Q = 64
        D_V = 64
        D_MODEL = 128

        def _trunc_normal(key, shape, std):
            return jax.random.truncated_normal(key, -3.0, 3.0, shape, dtype=jnp.float32) * std
        key = jax.random.key(seed)
        k_x, k_q, k_k, k_v, k_o = jax.random.split(key, 5)

        def init_w(k, out_f, in_f):
            s = np.sqrt(2.0 / (in_f + out_f))
            return _trunc_normal(k, (out_f, in_f), s)
        return {'in_features': jax.random.normal(k_x, (4, 256, D_ATT_IN), dtype=jnp.float32), 'w_q': init_w(k_q, NUM_HEADS * D_Q, D_ATT_IN), 'w_k': init_w(k_k, NUM_HEADS * D_Q, D_ATT_IN), 'w_v': init_w(k_v, NUM_HEADS * D_V, D_ATT_IN), 'w_o': init_w(k_o, D_MODEL, NUM_HEADS * D_V)}
    _L3_attn_in = _L3_attn_setup()

    def _L3_ffn_setup():
        import jax, jax.numpy as jnp
        import numpy as np

        def _binarize(w):
            alpha = jax.lax.stop_gradient(jnp.mean(jnp.abs(w), axis=1, keepdims=True))
            bw = alpha * jnp.sign(w)
            return w + jax.lax.stop_gradient(bw - w)
        key = jax.random.key(seed)
        k1, k2, k3, k4, k5 = jax.random.split(key, 5)
        D, H = (128, 512)
        x = jax.random.normal(k1, (64, 196, D), dtype=jnp.float32)
        w1 = jax.random.normal(k2, (H, D), dtype=jnp.float32) * 0.02
        b1 = jax.random.normal(k3, (H,), dtype=jnp.float32) * 0.02
        w2 = jax.random.normal(k4, (D, H), dtype=jnp.float32) * 0.02
        b2 = jax.random.normal(k5, (D,), dtype=jnp.float32) * 0.02
        return {'x': x, 'w1': w1, 'b1': b1, 'w2': w2, 'b2': b2}
    _L3_ffn_in = _L3_ffn_setup()
    _L3_c = _w((lambda *s: np.random.randn(*s).astype(np.float32) * 0.05)(16, 128))
    _L3_wmod = _w((lambda *s: np.random.randn(*s).astype(np.float32) * 0.05)(128, 6 * 128) * 128 ** (-0.5))
    _d = {'L0_attn_x': _L0_attn_in['x'], 'L0_attn_W_in': _L0_attn_in['W_in'], 'L0_attn_b_in': _L0_attn_in['b_in'], 'L0_attn_conv_k': _L0_attn_in['conv_k'], 'L0_attn_conv_b': _L0_attn_in['conv_b'], 'L0_attn_A_log': _L0_attn_in['A_log'], 'L0_attn_W_xp': _L0_attn_in['W_xp'], 'L0_attn_b_xp': _L0_attn_in['b_xp'], 'L0_attn_W_dt': _L0_attn_in['W_dt'], 'L0_attn_b_dt': _L0_attn_in['b_dt'], 'L0_attn_D_ssm': _L0_attn_in['D_ssm'], 'L0_attn_W_out': _L0_attn_in['W_out'], 'L0_attn_b_out': _L0_attn_in['b_out'], 'L0_ffn_w_gate': _L0_ffn_in['w_gate'], 'L0_ffn_w_up': _L0_ffn_in['w_up'], 'L0_ffn_w_down': _L0_ffn_in['w_down'], 'L0_c': _L0_c, 'L0_wmod': _L0_wmod, 'L1_attn_Wq': _L1_attn_in['Wq'], 'L1_attn_bq': _L1_attn_in['bq'], 'L1_attn_Wk': _L1_attn_in['Wk'], 'L1_attn_bk': _L1_attn_in['bk'], 'L1_attn_Wv': _L1_attn_in['Wv'], 'L1_attn_bv': _L1_attn_in['bv'], 'L1_attn_Wo': _L1_attn_in['Wo'], 'L1_attn_bo': _L1_attn_in['bo'], 'L1_attn_lq1': _L1_attn_in['lq1'], 'L1_attn_lk1': _L1_attn_in['lk1'], 'L1_attn_lq2': _L1_attn_in['lq2'], 'L1_attn_lk2': _L1_attn_in['lk2'], 'L1_attn_gn_w': _L1_attn_in['gn_w'], 'L1_attn_gn_b': _L1_attn_in['gn_b'], 'L1_ffn_Wqkv': _L1_ffn_in['Wqkv'], 'L1_ffn_q_scale': _L1_ffn_in['q_scale'], 'L1_ffn_k_scale': _L1_ffn_in['k_scale'], 'L1_ffn_Wo': _L1_ffn_in['Wo'], 'L1_ffn_ln_g': _L1_ffn_in['ln_g'], 'L1_ffn_ln_b': _L1_ffn_in['ln_b'], 'L1_ffn_W1': _L1_ffn_in['W1'], 'L1_ffn_b1': _L1_ffn_in['b1'], 'L1_ffn_W2': _L1_ffn_in['W2'], 'L1_ffn_b2': _L1_ffn_in['b2'], 'L1_c': _L1_c, 'L1_wmod': _L1_wmod, 'L2_attn_Wq': _L2_attn_in['Wq'], 'L2_attn_bq': _L2_attn_in['bq'], 'L2_attn_Wk': _L2_attn_in['Wk'], 'L2_attn_bk': _L2_attn_in['bk'], 'L2_attn_Wv': _L2_attn_in['Wv'], 'L2_attn_bv': _L2_attn_in['bv'], 'L2_attn_Wo': _L2_attn_in['Wo'], 'L2_attn_bo': _L2_attn_in['bo'], 'L2_ffn_router_w': _L2_ffn_in['router_w'], 'L2_ffn_router_b': _L2_ffn_in['router_b'], 'L2_ffn_routed_w1': _L2_ffn_in['routed_w1'], 'L2_ffn_routed_w3': _L2_ffn_in['routed_w3'], 'L2_ffn_routed_w2': _L2_ffn_in['routed_w2'], 'L2_ffn_shared_w1': _L2_ffn_in['shared_w1'], 'L2_ffn_shared_w3': _L2_ffn_in['shared_w3'], 'L2_ffn_shared_w2': _L2_ffn_in['shared_w2'], 'L2_c': _L2_c, 'L2_wmod': _L2_wmod, 'L3_attn_w_q': _L3_attn_in['w_q'], 'L3_attn_w_k': _L3_attn_in['w_k'], 'L3_attn_w_v': _L3_attn_in['w_v'], 'L3_attn_w_o': _L3_attn_in['w_o'], 'L3_ffn_w1': _L3_ffn_in['w1'], 'L3_ffn_b1': _L3_ffn_in['b1'], 'L3_ffn_w2': _L3_ffn_in['w2'], 'L3_ffn_b2': _L3_ffn_in['b2'], 'L3_c': _L3_c, 'L3_wmod': _L3_wmod}
    _x0 = _d['L0_attn_x']
    _d['L0_attn_x'] = jax.random.normal(jax.random.fold_in(jax.random.key(seed), 1), (16, 256, 128), dtype=_x0.dtype)
    del _x0
    return _d

def reference(L0_attn_x, L0_attn_W_in, L0_attn_b_in, L0_attn_conv_k, L0_attn_conv_b, L0_attn_A_log, L0_attn_W_xp, L0_attn_b_xp, L0_attn_W_dt, L0_attn_b_dt, L0_attn_D_ssm, L0_attn_W_out, L0_attn_b_out, L0_ffn_w_gate, L0_ffn_w_up, L0_ffn_w_down, L0_c, L0_wmod, L1_attn_Wq, L1_attn_bq, L1_attn_Wk, L1_attn_bk, L1_attn_Wv, L1_attn_bv, L1_attn_Wo, L1_attn_bo, L1_attn_lq1, L1_attn_lk1, L1_attn_lq2, L1_attn_lk2, L1_attn_gn_w, L1_attn_gn_b, L1_ffn_Wqkv, L1_ffn_q_scale, L1_ffn_k_scale, L1_ffn_Wo, L1_ffn_ln_g, L1_ffn_ln_b, L1_ffn_W1, L1_ffn_b1, L1_ffn_W2, L1_ffn_b2, L1_c, L1_wmod, L2_attn_Wq, L2_attn_bq, L2_attn_Wk, L2_attn_bk, L2_attn_Wv, L2_attn_bv, L2_attn_Wo, L2_attn_bo, L2_ffn_router_w, L2_ffn_router_b, L2_ffn_routed_w1, L2_ffn_routed_w3, L2_ffn_routed_w2, L2_ffn_shared_w1, L2_ffn_shared_w3, L2_ffn_shared_w2, L2_c, L2_wmod, L3_attn_w_q, L3_attn_w_k, L3_attn_w_v, L3_attn_w_o, L3_ffn_w1, L3_ffn_b1, L3_ffn_w2, L3_ffn_b2, L3_c, L3_wmod):

    def _L0_attn_ref(x, W_in, b_in, conv_k, conv_b, A_log, W_xp, b_xp, W_dt, b_dt, D_ssm, W_out, b_out):
        import jax, jax.numpy as jnp
        import numpy as np
        from functools import partial
        DIM, D_STATE, D_CONV, EXPAND = (128, 16, 4, 2)
        D_INNER = DIM * EXPAND
        DT_RANK = max(1, D_INNER // 16)
        B_SZ, L = (4, 256)

        def _mamba_fwd(x, W_in, b_in, conv_k, conv_b, A_log, W_xp, b_xp, W_dt, b_dt, D_ssm, W_out, b_out):
            xz = x @ W_in + b_in
            x_proj, z = jnp.split(xz, 2, axis=-1)
            x_conv = jax.lax.conv_general_dilated(x_proj, conv_k, window_strides=(1,), padding=[(D_CONV - 1, 0)], dimension_numbers=('NWC', 'WIO', 'NWC'), feature_group_count=D_INNER) + conv_b
            xa = jax.nn.silu(x_conv)
            dtBC = xa @ W_xp + b_xp
            dt_int, B_c, C_c = jnp.split(dtBC, [DT_RANK, DT_RANK + D_STATE], axis=-1)
            dt = jax.nn.softplus(dt_int @ W_dt + b_dt)
            A = -jnp.exp(A_log)

            def step(h, inp):
                x_t, dt_t, B_t, C_t = inp
                A_bar = jnp.exp(dt_t[..., None] * A)
                h = A_bar * h + dt_t[..., None] * B_t[:, None, :] * x_t[..., None]
                y_t = jnp.sum(C_t[:, None, :] * h, axis=-1)
                return (h, y_t)
            h0 = jnp.zeros((x.shape[0], D_INNER, D_STATE), x.dtype)
            tm = lambda a: jnp.swapaxes(a, 0, 1)
            _, y = jax.lax.scan(step, h0, (tm(xa), tm(dt), tm(B_c), tm(C_c)))
            y = jnp.swapaxes(y, 0, 1) + xa * D_ssm
            return y * jax.nn.silu(z) @ W_out + b_out
        return _mamba_fwd(x, W_in, b_in, conv_k, conv_b, A_log, W_xp, b_xp, W_dt, b_dt, D_ssm, W_out, b_out)

    def _L0_ffn_ref(x, w_gate, w_up, w_down):
        import jax, jax.numpy as jnp
        import numpy as np
        BLOCK = 16
        _GRID = jnp.array([0.0, 0.5, 1.0, 1.5, 2.0, 3.0, 4.0, 6.0], dtype=jnp.float32)
        _MID = jnp.array([0.25, 0.75, 1.25, 1.75, 2.5, 3.5, 5.0], dtype=jnp.float32)

        def fp4_quant_dequant(x):
            shape = x.shape
            xb = x.reshape(shape[:-1] + (shape[-1] // BLOCK, BLOCK))
            scale = jnp.max(jnp.abs(xb), axis=-1, keepdims=True) / 6.0
            scale = jnp.maximum(scale, jnp.float32(1e-12))
            xn = xb / scale
            idx = jnp.searchsorted(_MID, jnp.abs(xn))
            q = _GRID[idx] * jnp.sign(xn) * scale
            return q.reshape(shape)

        def fp4_linear(x, w):
            xq = fp4_quant_dequant(x)
            wq = fp4_quant_dequant(w)
            return jnp.einsum('bsk,nk->bsn', xq, wq)
        gate = fp4_linear(x, w_gate)
        y = fp4_linear(x, w_up)
        h = jax.nn.silu(gate) * y
        return fp4_linear(h, w_down)

    def _L1_attn_ref(x, Wq, bq, Wk, bk, Wv, bv, Wo, bo, lq1, lk1, lq2, lk2, gn_w, gn_b):
        import jax, jax.numpy as jnp
        import numpy as np
        B, S, D, H = (2, 256, 128, 16)
        DH = D // H
        EPS = 1e-05
        LAMBDA_INIT = 0.8
        b, s, d = x.shape
        h, dh = lq1.shape
        scale = dh ** (-0.5)
        q = (x @ Wq + bq).reshape(b, s, h, dh)
        k = (x @ Wk + bk).reshape(b, s, h, dh)
        v = (x @ Wv + bv).reshape(b, s, h, dh)
        lam = jnp.exp((lq1 * lk1).sum(-1)) - jnp.exp((lq2 * lk2).sum(-1)) + LAMBDA_INIT
        scores = jnp.einsum('bihd,bjhd->bhij', q, k) * scale * lam[None, :, None, None]
        attn = jax.nn.softmax(scores, axis=-1)
        out = jnp.einsum('bhij,bjhd->bihd', attn, v)
        mean = out.mean(axis=(1, 3), keepdims=True)
        var = out.var(axis=(1, 3), keepdims=True)
        normed = (out - mean) * jax.lax.rsqrt(var + EPS)
        normed = normed * gn_w[None, None, :, :] + gn_b[None, None, :, :]
        y = normed.reshape(b, s, d) @ Wo + bo
        return y

    def _L1_ffn_ref(x, Wqkv, q_scale, k_scale, Wo, ln_g, ln_b, W1, b1, W2, b2):
        import jax, jax.numpy as jnp
        import numpy as np
        DIM = 128
        DEPTH = 6
        HEADS = 16
        DIM_HEAD = 64
        WINDOW = 32
        INNER = HEADS * DIM_HEAD
        DIM_INNER = int(DIM * 4 * 2 / 3)
        QK_SCALE = 8.0

        def shift_tokens(t):
            a, s = jnp.split(t, 2, -1)
            s = jnp.pad(s, ((0, 0), (1, 0), (0, 0)))[:, :-1]
            return jnp.concatenate([a, s], -1)

        def l2norm(t):
            return t / jnp.maximum(jnp.linalg.norm(t, axis=-1, keepdims=True), 1e-12)

        def rotate_half(x):
            x1, x2 = jnp.split(x, 2, -1)
            return jnp.concatenate([-x2, x1], -1)

        def rotary_tables(n):
            half = jnp.arange(0, DIM_HEAD, 2, dtype=jnp.float32)
            inv_freq = 1.0 / 10000.0 ** (half / DIM_HEAD)
            t = jnp.arange(n, dtype=jnp.float32)
            freqs = t[:, None] * inv_freq[None, :]
            freqs = jnp.concatenate([freqs, freqs], -1)
            base_scale = (half + 0.4 * DIM_HEAD) / (1.4 * DIM_HEAD)
            power = (t - n // 2) / (WINDOW // 2)
            scale = base_scale[None, :] ** power[:, None]
            scale = jnp.concatenate([scale, scale], -1)
            return (freqs, scale)

        def local_attention(q, k, v):
            b, h, n, d = q.shape
            w = WINDOW
            nw = n // w
            bq = q.reshape(b, h, nw, w, d)
            bk = k.reshape(b, h, nw, w, d)
            bv = v.reshape(b, h, nw, w, d)

            def look(t):
                p = jnp.pad(t, ((0, 0), (0, 0), (1, 0), (0, 0), (0, 0)))
                return jnp.concatenate([p[:, :, :nw], p[:, :, 1:]], axis=3)
            bk2, bv2 = (look(bk), look(bv))
            seq = jnp.arange(n).reshape(nw, w)
            seq_p = jnp.pad(seq, ((1, 0), (0, 0)), constant_values=-1)
            jt = jnp.concatenate([seq_p[:nw], seq_p[1:]], axis=1)
            it = seq[:, :, None]
            jb = jt[:, None, :]
            mask = (it < jb) | (it > jb + w) | (jb == -1)
            sim = jnp.einsum('bhwie,bhwje->bhwij', bq, bk2) * QK_SCALE
            sim = jnp.where(mask, -jnp.finfo(sim.dtype).max, sim)
            attn = jax.nn.softmax(sim, -1)
            out = jnp.einsum('bhwij,bhwje->bhwie', attn, bv2)
            return out.reshape(b, h, n, d)

        def attn_layer(x, Wqkv, qs, ksc, Wo):
            b, n, _ = x.shape
            qkv = x @ Wqkv
            q, k, v = jnp.split(qkv, 3, -1)
            sh = lambda t: t.reshape(b, n, HEADS, DIM_HEAD).transpose(0, 2, 1, 3)
            q, k, v = (sh(q), sh(k), sh(v))
            q = l2norm(q) * qs
            k = l2norm(k) * ksc
            freqs, scale = rotary_tables(n)
            cos, sin = (jnp.cos(freqs), jnp.sin(freqs))
            q = q * cos * scale + rotate_half(q) * sin * scale
            inv = 1.0 / scale
            k = k * cos * inv + rotate_half(k) * sin * inv
            out = local_attention(q, k, v)
            out = out.transpose(0, 2, 1, 3).reshape(b, n, INNER)
            return out @ Wo

        def ffn_layer(x, g, bln, W1, b1, W2, b2):
            mu = x.mean(-1, keepdims=True)
            var = ((x - mu) ** 2).mean(-1, keepdims=True)
            xn = (x - mu) / jnp.sqrt(var + 1e-05) * g + bln
            hg = xn @ W1 + b1
            a, gate = jnp.split(hg, 2, -1)
            return a * jax.nn.gelu(gate, approximate=False) @ W2 + b2
        for i in range(DEPTH):
            x = attn_layer(shift_tokens(x), Wqkv[i], q_scale[i], k_scale[i], Wo[i]) + x
            x = ffn_layer(shift_tokens(x), ln_g[i], ln_b[i], W1[i], b1[i], W2[i], b2[i]) + x
        return x

    def _L2_attn_ref(x, Wq, bq, Wk, bk, Wv, bv, Wo, bo):
        import jax, jax.numpy as jnp
        import numpy as np
        D_MODEL = 128
        N_HEADS = 16
        N_GROUPS = 4
        D_HEAD = D_MODEL // N_HEADS
        HPG = N_HEADS // N_GROUPS
        B, T = (2, 256)

        def _rope(x):
            t, d = (x.shape[2], x.shape[3])
            pos = jnp.arange(t, dtype=jnp.float32)[:, None]
            freq = jnp.exp(-(jnp.arange(0, d, 2, dtype=jnp.float32) / d) * jnp.log(jnp.float32(10000.0)))
            angle = pos * freq
            cos, sin = (jnp.cos(angle), jnp.sin(angle))
            xe, xo = (x[..., ::2], x[..., 1::2])
            re = xe * cos - xo * sin
            ro = xe * sin + xo * cos
            return jnp.stack([re, ro], axis=-1).reshape(x.shape)
        b, t, _ = x.shape
        q = (x @ Wq + bq).reshape(b, t, N_HEADS, D_HEAD).transpose(0, 2, 1, 3)
        k = (x @ Wk + bk).reshape(b, t, N_GROUPS, D_HEAD).transpose(0, 2, 1, 3)
        v = (x @ Wv + bv).reshape(b, t, N_GROUPS, D_HEAD).transpose(0, 2, 1, 3)
        k = jnp.repeat(k, HPG, axis=1)
        v = jnp.repeat(v, HPG, axis=1)
        q = _rope(q)
        k = _rope(k)
        scale = jnp.float32(np.sqrt(D_HEAD))
        scores = jnp.einsum('bhtd,bhsd->bhts', q, k) / scale
        causal = jnp.tril(jnp.ones((t, t), dtype=bool))
        scores = jnp.where(causal, scores, -jnp.inf)
        probs = jax.nn.softmax(scores, axis=-1)
        attn = jnp.einsum('bhts,bhsd->bhtd', probs, v)
        out = attn.transpose(0, 2, 1, 3).reshape(b, t, N_HEADS * D_HEAD)
        return out @ Wo + bo

    def _L2_ffn_ref(x, router_w, router_b, routed_w1, routed_w3, routed_w2, shared_w1, shared_w3, shared_w2):
        import jax, jax.numpy as jnp
        import numpy as np
        BEST_K = 2

        def _expert(xf, w1, w3, w2):
            return jax.nn.silu(xf @ w1) * (xf @ w3) @ w2
        B, S, D = x.shape
        T = B * S
        xf = x.reshape(T, D)
        logits = xf @ router_w + router_b
        topk_vals, topk_idx = jax.lax.top_k(logits, BEST_K)
        sparse = jnp.full_like(logits, -jnp.inf)
        sparse = sparse.at[jnp.arange(T)[:, None], topk_idx].set(topk_vals)
        gates = jax.nn.softmax(sparse, axis=-1)
        routed = jax.vmap(_expert, in_axes=(None, 0, 0, 0))(xf, routed_w1, routed_w3, routed_w2)
        routed_out = jnp.einsum('etd,te->td', routed, gates)
        shared_out = jax.vmap(_expert, in_axes=(None, 0, 0, 0))(xf, shared_w1, shared_w3, shared_w2).sum(axis=0)
        return (routed_out + shared_out).reshape(B, S, D)

    def _L3_attn_ref(in_features, w_q, w_k, w_v, w_o):
        import jax, jax.numpy as jnp
        import numpy as np
        D_ATT_IN = 128
        NUM_HEADS = 16
        D_Q = 64
        D_V = 64
        D_MODEL = 128

        def _trunc_normal(key, shape, std):
            return jax.random.truncated_normal(key, -3.0, 3.0, shape, dtype=jnp.float32) * std
        q = jnp.einsum('oi,bsi->bso', w_q, in_features)
        k = jnp.einsum('oi,bsi->bso', w_k, in_features)
        v = jnp.einsum('oi,bsi->bso', w_v, in_features)
        s = in_features.shape[-2]
        scores = jnp.einsum('bqd,bkd->bqk', q, k) / jnp.sqrt(jnp.asarray(k.shape[-1], q.dtype))
        causal = jnp.tril(jnp.ones((s, s), dtype=bool))
        scores = jnp.where(causal[None, :, :], scores, -jnp.inf)
        att = jax.nn.softmax(scores, axis=-1)
        ctx = jnp.einsum('bqk,bkd->bqd', att, v)
        return jnp.einsum('oi,bsi->bso', w_o, ctx)

    def _L3_ffn_ref(x, w1, b1, w2, b2):
        import jax, jax.numpy as jnp
        import numpy as np

        def _binarize(w):
            alpha = jax.lax.stop_gradient(jnp.mean(jnp.abs(w), axis=1, keepdims=True))
            bw = alpha * jnp.sign(w)
            return w + jax.lax.stop_gradient(bw - w)
        bw1 = _binarize(w1)
        h = jnp.einsum('bsd,hd->bsh', x, bw1) + b1
        h = jax.nn.gelu(h, approximate=False)
        bw2 = _binarize(w2)
        out = jnp.einsum('bsh,dh->bsd', h, bw2) + b2
        return out
    x = L0_attn_x
    mod = (_silu(L0_c) @ L0_wmod).reshape(L0_c.shape[0], 6, 1, -1)
    sa, ca, ga, sb, cb, gb = (mod[:, 0], mod[:, 1], mod[:, 2], mod[:, 3], mod[:, 4], mod[:, 5])
    ga = (2 * (ga >= 0) - 1) * jnp.maximum(jnp.abs(ga), 0.25)
    gb = (2 * (gb >= 0) - 1) * jnp.maximum(jnp.abs(gb), 0.25)
    h = _layernorm(x, axis=-1) * (1 + ca) + sa
    x = x + ga * _L0_attn_ref(h, L0_attn_W_in, L0_attn_b_in, L0_attn_conv_k, L0_attn_conv_b, L0_attn_A_log, L0_attn_W_xp, L0_attn_b_xp, L0_attn_W_dt, L0_attn_b_dt, L0_attn_D_ssm, L0_attn_W_out, L0_attn_b_out)
    h = _layernorm(x, axis=-1) * (1 + cb) + sb
    x = x + gb * _L0_ffn_ref(h, L0_ffn_w_gate, L0_ffn_w_up, L0_ffn_w_down)
    mod = (_silu(L1_c) @ L1_wmod).reshape(L1_c.shape[0], 6, 1, -1)
    sa, ca, ga, sb, cb, gb = (mod[:, 0], mod[:, 1], mod[:, 2], mod[:, 3], mod[:, 4], mod[:, 5])
    ga = (2 * (ga >= 0) - 1) * jnp.maximum(jnp.abs(ga), 0.25)
    gb = (2 * (gb >= 0) - 1) * jnp.maximum(jnp.abs(gb), 0.25)
    h = _layernorm(x, axis=-1) * (1 + ca) + sa
    x = x + ga * _L1_attn_ref(h, L1_attn_Wq, L1_attn_bq, L1_attn_Wk, L1_attn_bk, L1_attn_Wv, L1_attn_bv, L1_attn_Wo, L1_attn_bo, L1_attn_lq1, L1_attn_lk1, L1_attn_lq2, L1_attn_lk2, L1_attn_gn_w, L1_attn_gn_b)
    h = _layernorm(x, axis=-1) * (1 + cb) + sb
    x = x + gb * _L1_ffn_ref(h, L1_ffn_Wqkv, L1_ffn_q_scale, L1_ffn_k_scale, L1_ffn_Wo, L1_ffn_ln_g, L1_ffn_ln_b, L1_ffn_W1, L1_ffn_b1, L1_ffn_W2, L1_ffn_b2)
    mod = (_silu(L2_c) @ L2_wmod).reshape(L2_c.shape[0], 6, 1, -1)
    sa, ca, ga, sb, cb, gb = (mod[:, 0], mod[:, 1], mod[:, 2], mod[:, 3], mod[:, 4], mod[:, 5])
    ga = (2 * (ga >= 0) - 1) * jnp.maximum(jnp.abs(ga), 0.25)
    gb = (2 * (gb >= 0) - 1) * jnp.maximum(jnp.abs(gb), 0.25)
    h = _layernorm(x, axis=-1) * (1 + ca) + sa
    x = x + ga * _L2_attn_ref(h, L2_attn_Wq, L2_attn_bq, L2_attn_Wk, L2_attn_bk, L2_attn_Wv, L2_attn_bv, L2_attn_Wo, L2_attn_bo)
    h = _layernorm(x, axis=-1) * (1 + cb) + sb
    x = x + gb * _L2_ffn_ref(h, L2_ffn_router_w, L2_ffn_router_b, L2_ffn_routed_w1, L2_ffn_routed_w3, L2_ffn_routed_w2, L2_ffn_shared_w1, L2_ffn_shared_w3, L2_ffn_shared_w2)
    mod = (_silu(L3_c) @ L3_wmod).reshape(L3_c.shape[0], 6, 1, -1)
    sa, ca, ga, sb, cb, gb = (mod[:, 0], mod[:, 1], mod[:, 2], mod[:, 3], mod[:, 4], mod[:, 5])
    ga = (2 * (ga >= 0) - 1) * jnp.maximum(jnp.abs(ga), 0.25)
    gb = (2 * (gb >= 0) - 1) * jnp.maximum(jnp.abs(gb), 0.25)
    h = _layernorm(x, axis=-1) * (1 + ca) + sa
    x = x + ga * _L3_attn_ref(h, L3_attn_w_q, L3_attn_w_k, L3_attn_w_v, L3_attn_w_o)
    h = _layernorm(x, axis=-1) * (1 + cb) + sb
    x = x + gb * _L3_ffn_ref(h, L3_ffn_w1, L3_ffn_b1, L3_ffn_w2, L3_ffn_b2)
    return x

_drawn_inputs = setup_inputs


def setup_inputs(seed=0):
    import zlib

    import numpy as np

    out = dict(_drawn_inputs(seed))
    spreads = {'L0_attn_b_in': (0.0, 0.789),
     'L0_attn_conv_b': (0.0, 0.637),
     'L0_attn_b_xp': (0.0, 0.8),
     'L0_attn_D_ssm': (1.0, 0.6),
     'L0_attn_b_out': (0.0, 0.1),
     'L1_attn_gn_w': (1.0, 0.2),
     'L1_attn_gn_b': (0.0, 0.399),
     'L1_ffn_q_scale': (1.0, 0.6),
     'L1_ffn_k_scale': (1.0, 0.6),
     'L1_ffn_ln_g': (1.0, 0.6),
     'L1_ffn_ln_b': (0.0, 0.8),
     'L1_ffn_b1': (0.0, 0.8),
     'L1_ffn_b2': (0.0, 0.648),
     'L2_ffn_router_b': (0.0, 2.0)}
    factors = {'L0_attn_A_log': 8.0,
     'L0_attn_W_dt': 7.282,
     'L0_attn_b_dt': 8.0,
     'L0_ffn_w_gate': 8.0,
     'L0_ffn_w_up': 8.0,
     'L0_ffn_w_down': 8.0,
     'L1_attn_bq': 28.365,
     'L1_attn_bk': 64.0,
     'L1_attn_bo': 8.0,
     'L1_ffn_W1': 7.768,
     'L1_ffn_W2': 7.623,
     'L2_attn_Wq': 8.0,
     'L2_attn_bq': 64.0,
     'L2_attn_Wk': 8.0,
     'L2_attn_bk': 64.0,
     'L2_attn_Wv': 8.0,
     'L2_attn_bv': 59.803,
     'L2_attn_Wo': 8.0,
     'L2_attn_bo': 64.0,
     'L2_ffn_router_w': 8.0,
     'L2_ffn_routed_w1': 8.0,
     'L2_ffn_routed_w3': 8.0,
     'L2_ffn_routed_w2': 8.0,
     'L2_ffn_shared_w1': 8.0,
     'L2_ffn_shared_w3': 8.0,
     'L2_ffn_shared_w2': 8.0,
     'L2_c': 8.0,
     'L2_wmod': 8.0,
     'L3_attn_w_q': 45.826,
     'L3_attn_w_k': 45.585,
     'L3_ffn_w1': 7.208,
     'L3_ffn_b1': 64.0,
     'L3_ffn_w2': 6.998,
     'L3_ffn_b2': 64.0,
     'L1_attn_bv': 3.439,
     'L3_attn_w_v': 4.845,
     'L3_attn_w_o': 4.789}
    for name, (base, spread) in spreads.items():
        noise = np.random.default_rng([zlib.crc32(name.encode()), seed]).standard_normal(out[name].shape)
        drawn = base * np.exp(spread * noise) if base else spread * noise
        out[name] = jnp.asarray(drawn.astype(out[name].dtype))
    for name, factor in factors.items():
        out[name] = (out[name] * factor).astype(out[name].dtype)
    return out
```

```python
from contextlib import ExitStack

import numpy as np

import concourse.bass as bass
from concourse import mybir

P = 128
ALU = mybir.AluOpType
ACT = mybir.ActivationFunctionType
AX = mybir.AxisListType
F32 = mybir.dt.float32
BF16 = mybir.dt.bfloat16
I32 = mybir.dt.int32
LAYERS = 4
LN_EPS = 1e-5
SHIFT_A, SCALE_A, GATE_A, SHIFT_B, SCALE_B, GATE_B = range(6)


class Signals:

    def __init__(self, nc, ctx, prefix):
        self.nc, self.prefix, self.made = nc, prefix, {}
        ctx.callback(self.clear)

    def __getitem__(self, name):
        if name not in self.made:
            self.made[name] = self.nc.alloc_semaphore(name=f"{self.prefix}_{name}")
        return self.made[name]

    def clear(self):
        self.nc.clear_and_free_semaphores(list(self.made.values()))
        self.nc.all_engine_barrier()


class Core:
    pass


def open_core(nc, ctx, x_in):
    core = Core()
    core.nc, core.ctx = nc, ctx
    core.B, core.S, core.D = x_in.shape

    def sb(name, shape, dt=F32):
        return ctx.enter_context(nc.sbuf_tensor(name, shape, dt))

    core.x = sb("x", [P, core.B, core.S])
    core.mod = sb("mod", [P, LAYERS, 6, core.B])
    core.ident = sb("ident", [P, P])
    core.mean_w = sb("mean_w", [P, P])
    core.eps = sb("eps", [P, 1])
    return core


def stage_load(core, T):
    nc, B, S = core.nc, core.B, core.S
    TT = B * S // P
    with ExitStack() as ctx:
        sg = Signals(nc, ctx, "ld")

        def sb(name, shape, dt=F32):
            return ctx.enter_context(nc.sbuf_tensor(name, shape, dt))

        xin = sb("xin", [P, TT, P])
        cT = sb("cT", [P, LAYERS, B])
        silu = sb("silu", [P, LAYERS, B])
        den = sb("den", [P, LAYERS, B])
        wmod = sb("wmod", [P, LAYERS, 6 * P])
        gsign = sb("gsign", [P, LAYERS, 2, B])
        gabs = sb("gabs", [P, LAYERS, 2, B])
        graw = sb("graw", [P, LAYERS, 2, B])
        ps_x = ctx.enter_context(nc.psum_tensor("ps_x", [P, 2, 4, P], F32))
        ps_m = ctx.enter_context(nc.psum_tensor("ps_m", [P, LAYERS * 6 * B], F32))
        x_flat = core.x[:, :, :].rearrange("p b s -> p (b s)")
        mods = ps_m[:, :].rearrange("p (l m b) -> p l m b", l=LAYERS, m=6)
        groups = TT // 4
        block = ctx.enter_context(nc.Block())

        @block.sync
        def _(sp):
            sp.dma_start(xin[:, :, :], T["L0_attn_x"].rearrange("b (t p) d -> p (b t) d", p=P)).then_inc(sg["x_in"], 16)
            for l in range(LAYERS):
                sp.dma_start(wmod[:, l, :], T[f"L{l}_wmod"]).then_inc(sg["w_in"], 16)

        @block.scalar
        def _(act):
            for l in range(LAYERS):
                with nc.allow_non_contiguous_dma("small"):
                    act.dma_start(cT[:, l, :], T[f"L{l}_c"].rearrange("b d -> d b")).then_inc(sg["c_in"], 16)
            act.wait_ge(sg["c_in"], 16 * LAYERS)
            nc.scalar.activation(den[:, :, :], cT[:, :, :], ACT.Exp, scale=-1.0).then_inc(sg["exp"], 1)

        @block.gpsimd
        def _(pool):
            pool.memset(core.ident[:, :], 0.0).then_inc(sg["zero"], 1)
            pool.memset(core.mean_w[:, :], 1.0 / P).then_inc(sg["const"], 1)
            pool.memset(core.eps[:, :], LN_EPS).then_inc(sg["const"], 1)
            pool.wait_ge(sg["zero"], 1)
            pool.affine_select(out=core.ident[:, :], in_=core.ident[:, :], compare_op=ALU.not_equal, fill=1.0,
                               base=0, pattern=[[-1, P]], channel_multiplier=1).then_inc(sg["ident"], 1)

        @block.tensor
        def _(pe):
            pe.wait_ge(sg["ident"], 1)
            pe.wait_ge(sg["x_in"], 16)
            for g in range(groups):
                if g >= 2:
                    pe.wait_ge(sg["x_copied"], g - 1)
                for t in range(4):
                    last = pe.transpose(ps_x[:, g % 2, t, :], xin[:, 4 * g + t, :], core.ident[:, :])
                last.then_inc(sg["x_turned"], 1)
            pe.wait_ge(sg["silu"], 1)
            pe.wait_ge(sg["w_in"], 16 * LAYERS)
            for l in range(LAYERS):
                for m in range(6):
                    last = pe.matmul(mods[:, l, m, :], wmod[:, l, m * P:(m + 1) * P], silu[:, l, :], start=True, stop=True)
            last.then_inc(sg["mods"], 1)

        @block.vector
        def _(dve):
            dve.wait_ge(sg["exp"], 1)
            nc.vector.tensor_scalar(den[:, :, :], den[:, :, :], 1.0, None, ALU.add).then_inc(sg["dve"], 1)
            dve.wait_ge(sg["dve"], 1)
            nc.vector.reciprocal(den[:, :, :], den[:, :, :]).then_inc(sg["dve"], 1)
            dve.wait_ge(sg["dve"], 2)
            nc.vector.tensor_tensor(silu[:, :, :], cT[:, :, :], den[:, :, :], ALU.mult).then_inc(sg["silu"], 1)
            for g in range(groups):
                dve.wait_ge(sg["x_turned"], g + 1)
                nc.vector.tensor_copy(x_flat[:, 4 * g * P:4 * (g + 1) * P],
                                      ps_x[:, g % 2, :, :].rearrange("p t c -> p (t c)")).then_inc(sg["x_copied"], 1)
            dve.wait_ge(sg["mods"], 1)
            for m in (SHIFT_A, SHIFT_B):
                nc.vector.tensor_copy(core.mod[:, :, m, :], mods[:, :, m, :])
            for m in (SCALE_A, SCALE_B):
                nc.vector.tensor_scalar(core.mod[:, :, m, :], mods[:, :, m, :], 1.0, None, ALU.add)
            nc.vector.tensor_copy(graw[:, :, 0, :], mods[:, :, GATE_A, :])
            nc.vector.tensor_copy(graw[:, :, 1, :], mods[:, :, GATE_B, :]).then_inc(sg["gate"], 1)
            dve.wait_ge(sg["gate"], 1)
            nc.vector.scalar_tensor_tensor(out=gabs[:, :, :, :].rearrange("p l k b -> p (l k b)"),
                                           in0=graw[:, :, :, :].rearrange("p l k b -> p (l k b)"), scalar=-1.0,
                                           in1=graw[:, :, :, :].rearrange("p l k b -> p (l k b)"), op0=ALU.mult, op1=ALU.max)
            nc.vector.tensor_scalar(gsign[:, :, :, :], graw[:, :, :, :], 0.0, 2.0, ALU.is_ge, ALU.mult).then_inc(sg["gate"], 1)
            dve.wait_ge(sg["gate"], 2)
            nc.vector.tensor_scalar(gsign[:, :, :, :], gsign[:, :, :, :], -1.0, None, ALU.add).then_inc(sg["gate"], 1)
            dve.wait_ge(sg["gate"], 3)
            for k, m in enumerate((GATE_A, GATE_B)):
                nc.vector.scalar_tensor_tensor(out=core.mod[:, :, m, :], in0=gabs[:, :, k, :], scalar=0.25,
                                               in1=gsign[:, :, k, :], op0=ALU.max, op1=ALU.mult)


def stage_store(core, out):
    nc, B, S = core.nc, core.B, core.S
    TT = B * S // P
    groups = TT // 4
    with ExitStack() as ctx:
        sg = Signals(nc, ctx, "st")
        xo = ctx.enter_context(nc.sbuf_tensor("xo", [P, TT, P], F32))
        ps_x = ctx.enter_context(nc.psum_tensor("ps_xo", [P, 2, 4, P], F32))
        x_flat = core.x[:, :, :].rearrange("p b s -> p (b s)")
        dst = out.rearrange("b (t p) d -> p (b t) d", p=P)
        block = ctx.enter_context(nc.Block())

        @block.tensor
        def _(pe):
            for g in range(groups):
                if g >= 2:
                    pe.wait_ge(sg["x_copied"], g - 1)
                for t in range(4):
                    c = 4 * g + t
                    last = pe.transpose(ps_x[:, g % 2, t, :], x_flat[:, c * P:(c + 1) * P], core.ident[:, :])
                last.then_inc(sg["x_turned"], 1)

        @block.vector
        def _(dve):
            for g in range(groups):
                dve.wait_ge(sg["x_turned"], g + 1)
                nc.vector.tensor_copy(xo[:, 4 * g:4 * g + 4, :], ps_x[:, g % 2, :, :]).then_inc(sg["x_copied"], 1)

        @block.sync
        def _(sp):
            for g in range(groups):
                sp.wait_ge(sg["x_copied"], g + 1)
                sp.dma_start(dst[:, 4 * g:4 * g + 4, :], xo[:, 4 * g:4 * g + 4, :]).then_inc(sg["stored"], 16)
            sp.wait_ge(sg["stored"], 16 * groups)



def wait(eng, sem, value):
    if not isinstance(value, int) or value > 0:
        eng.wait_ge(sem, value)


def pairs(eng, count, body):
    body(0, 0)
    if count > 1:
        body(1, 1)
    if count > 2:
        with eng.Fori(1, count // 2) as i:
            body(2 * i, 0)
            body(2 * i + 1, 1)


class AdaNorm:

    def __init__(self, core, ctx, sg, layer, shift, scale, buffers=None):
        nc = core.nc
        self.core, self.sg, self.layer, self.shift, self.scale = core, sg, layer, shift, scale
        self.items = core.B // 2
        W = self.W = 2 * core.S
        self.h = ctx.enter_context(nc.sbuf_tensor(f"h{layer}{shift}", [P, core.B, core.S], F32))
        self.cen, self.sq, self.rstd = buffers or [ctx.enter_context(nc.sbuf_tensor(f"{name}{layer}{shift}", [P, 2, W], F32))
                                                   for name in ("cen", "sq", "rstd")]
        self.ps_mean, self.ps_var = None, None

    def x_item(self, n):
        return self.core.x[:, bass.ds(2 * n, 2), :].rearrange("p b s -> p (b s)")

    def pe(self, pe):
        sg, core = self.sg, self.core

        def item(n, j):
            wait(pe, sg["ln_centered"], n - 1)
            pe.matmul(self.ps_mean[:, j, :], core.mean_w[:, :], self.x_item(n), start=True, stop=True).then_inc(sg["ln_mean"], 1)
            wait(pe, sg["ln_log"], n - 1)
            pe.wait_ge(sg["ln_square"], n + 1)
            pe.matmul(self.ps_var[:, j, :], core.mean_w[:, :], self.sq[:, j, :], start=True, stop=True).then_inc(sg["ln_var"], 1)

        pairs(pe, self.items, item)

    def act(self, act):
        nc, sg, core = self.core.nc, self.sg, self.core

        def item(n, j):
            act.wait_ge(sg["ln_centered"], n + 1)
            wait(act, sg["ln_var"], n - 1)
            nc.scalar.activation(self.sq[:, j, :], self.cen[:, j, :], ACT.Square).then_inc(sg["ln_square"], 1)
            act.wait_ge(sg["ln_var"], n + 1)
            wait(act, sg["ln_normed"], n - 1)
            nc.scalar.activation(self.rstd[:, j, :], self.ps_var[:, j, :], ACT.Ln, bias=core.eps[:, 0:1]).then_inc(sg["ln_log"], 1)
            act.wait_ge(sg["ln_log"], n + 1)
            nc.scalar.activation(self.rstd[:, j, :], self.rstd[:, j, :], ACT.Exp, scale=-0.5).then_inc(sg["ln_rstd"], 1)

        pairs(act, self.items, item)

    def dve(self, dve):
        nc, sg, core, S = self.core.nc, self.sg, self.core, self.core.S

        def finish(n, j):
            dve.wait_ge(sg["ln_rstd"], n + 1)
            h = self.h[:, bass.ds(2 * n, 2), :].rearrange("p b s -> p (b s)")
            nc.vector.tensor_tensor(h, self.cen[:, j, :], self.rstd[:, j, :], ALU.mult).then_inc(sg["ln_normed"], 1)
            dve.wait_ge(sg["ln_normed"], n + 1)
            for k in range(2):
                hb = self.h[:, bass.ds(2 * n + k, 1), :].rearrange("p b s -> p (b s)")
                last = nc.vector.tensor_scalar(hb, hb, core.mod[:, self.layer, self.scale, bass.ds(2 * n + k, 1)],
                                               core.mod[:, self.layer, self.shift, bass.ds(2 * n + k, 1)], ALU.mult, ALU.add)
            last.then_inc(sg["h"], 1)

        def item(n, j):
            dve.wait_ge(sg["ln_mean"], n + 1)
            wait(dve, sg["ln_square"], n - 1)
            nc.vector.tensor_tensor(self.cen[:, j, :], self.x_item(n), self.ps_mean[:, j, :], ALU.subtract).then_inc(sg["ln_centered"], 1)
            finish(n, j)

        pairs(dve, self.items, item)


def add_residual(core, sg, dve, n, tmp, b, layer, gate):
    xb = core.x[:, bass.ds(b, 1), :].rearrange("p b s -> p (b s)")
    return core.nc.vector.scalar_tensor_tensor(out=xb, in0=tmp, scalar=core.mod[:, layer, gate, bass.ds(b, 1)],
                                               in1=xb, op0=ALU.mult, op1=ALU.add)


def items_loop(eng, count, body):
    body(0, 0)
    if count > 1:
        with eng.Fori(1, count) as n:
            body(n, None)


class SmallHeads:

    H, DH = 16, 8

    def __init__(self, core, ctx, sg, name, causal, v_cols):
        nc, S = core.nc, core.S
        self.core, self.sg, self.causal, self.v_cols = core, sg, causal, v_cols

        def sb(n, shape, dt=F32):
            return ctx.enter_context(nc.sbuf_tensor(f"{name}_{n}", shape, dt))

        def psum(n, shape, dt=F32):
            return ctx.enter_context(nc.psum_tensor(f"{name}_{n}", shape, dt))

        self.q = sb("q", [P, 2, 4, S])
        self.k = sb("k", [P, 2, 4, S])
        self.v = sb("v", [P, 2, 2, v_cols])
        self.nmax = sb("nmax", [P, 2, self.H, 2])
        self.total = sb("total", [P, 2, self.H, 2])
        self.prob = sb("prob", [P, 3, 2, S])
        self.probT = sb("probT", [P, 2, 2, S])
        self.ps_s = psum("ps_s", [P, 3, 2, S])
        self.ps_t = psum("ps_t", [P, 2, 2, S])
        self.ps_o = psum("ps_o", [P, 2, self.H, self.DH])
        if causal:
            self.identb = sb("identb", [P, P], BF16)
            self.maskf = sb("maskf", [P, P])
            self.mask = sb("mask", [P, P], BF16)
        self.blocks = [(qt, kt) for qt in range(2) for kt in range(2) if not (causal and kt > qt)]

    def keys(self, qt):
        return self.core.S // 2 * (qt + 1) if self.causal else self.core.S

    def v_of(self, j, kt, h):
        c = h * self.DH if self.v_cols == P else (h // 4) * self.DH
        return self.v[:, j, kt, c:c + self.DH]

    def pool_consts(self, pool):
        sg, nc = self.sg, self.core.nc
        pool.memset(self.maskf[:, :], 0.0).then_inc(sg["mask0"], 1)
        pool.wait_ge(sg["mask0"], 1)
        pool.affine_select(out=self.maskf[:, :], in_=self.maskf[:, :], compare_op=ALU.is_ge, fill=-1e30,
                           base=0, pattern=[[-1, P]], channel_multiplier=1).then_inc(sg["mask0"], 1)
        pool.wait_ge(sg["mask0"], 2)
        pool.tensor_copy(self.mask[:, :], self.maskf[:, :]).then_inc(sg["mask"], 1)
        pool.tensor_copy(self.identb[:, :], self.core.ident[:, :]).then_inc(sg["mask"], 1)

    def pe(self, pe, n, j):
        sg, H = self.sg, self.H

        def scores(h):
            g, r = h // 4, 32 * (h % 4)
            wait(pe, sg["exp"], H * n + h - 2)
            for qt in range(2):
                ks = self.keys(qt)
                last = pe.matmul(self.ps_s[:, h % 3, qt, 0:ks], self.q[r:r + 8, j, g, qt * P:(qt + 1) * P],
                                 self.k[r:r + 8, j, g, 0:ks], start=True, stop=not self.causal, tile_position=(r, 0))
                if self.causal:
                    last = pe.matmul(self.ps_s[:, h % 3, qt, ks - P:ks], self.identb[:, :], self.mask[:, :],
                                     start=False, stop=True)
            last.then_inc(sg["scores"], 1)

        def turn(h):
            pe.wait_ge(sg["exp"], H * n + h + 1)
            wait(pe, sg["probT"], H * n + h - 1)
            for qt, kt in self.blocks:
                last = pe.transpose(self.ps_t[:, h % 2, kt, qt * P:(qt + 1) * P],
                                    self.prob[:, h % 3, qt, kt * P:(kt + 1) * P], self.core.ident[:, :])
            last.then_inc(sg["turned"], 1)

        def values(h):
            pe.wait_ge(sg["probT"], H * n + h + 1)
            if h == 0:
                wait(pe, sg["heads_out"], n)
            for qt in range(2):
                kts = [kt for a, kt in self.blocks if a == qt]
                for kt in kts:
                    last = pe.matmul(self.ps_o[:, qt, h, :], self.probT[:, h % 2, kt, qt * P:(qt + 1) * P],
                                     self.v_of(j, kt, h), start=(kt == kts[0]), stop=(kt == kts[-1]))
            last.then_inc(sg["values"], 1)

        for s in range(H + 3):
            if s < H:
                scores(s)
            if 2 <= s < H + 2:
                turn(s - 2)
            if s >= 3:
                values(s - 3)

    def dve(self, dve, n, j):
        nc, sg, H = self.core.nc, self.sg, self.H

        def copy(h):
            dve.wait_ge(sg["turned"], H * n + h + 1)
            wait(dve, sg["values"], H * n + h - 1)
            if self.causal:
                nc.vector.tensor_copy(self.probT[:, h % 2, 0, :], self.ps_t[:, h % 2, 0, :])
                nc.vector.tensor_copy(self.probT[:, h % 2, 1, P:2 * P], self.ps_t[:, h % 2, 1, P:2 * P]).then_inc(sg["probT"], 1)
            else:
                nc.vector.tensor_copy(self.probT[:, h % 2, :, :], self.ps_t[:, h % 2, :, :]).then_inc(sg["probT"], 1)

        for s in range(H + 2):
            if s < H:
                dve.wait_ge(sg["scores"], H * n + s + 1)
                if s == 0:
                    wait(dve, sg["exp"], H * (n - 1))
                if self.causal:
                    for qt in range(2):
                        last = nc.vector.tensor_reduce(self.nmax[:, j, s, qt:qt + 1], self.ps_s[:, s % 3, qt, 0:self.keys(qt)],
                                                       AX.X, ALU.max, negate=True)
                else:
                    last = nc.vector.tensor_reduce(self.nmax[:, j, s, :], self.ps_s[:, s % 3, :, :], AX.X, ALU.max, negate=True)
                last.then_inc(sg["max"], 1)
            if s >= 2:
                copy(s - 2)

    def act(self, act, n, j):
        nc, sg, H = self.core.nc, self.sg, self.H
        for h in range(H):
            act.wait_ge(sg["max"], H * n + h + 1)
            wait(act, sg["turned"], H * n + h - 2)
            if h == 0:
                wait(act, sg["heads_out"], n - 1)
            for qt in range(2):
                ks = self.keys(qt)
                last = nc.scalar.activation(self.prob[:, h % 3, qt, 0:ks], self.ps_s[:, h % 3, qt, 0:ks], ACT.Exp,
                                            bias=self.nmax[:, j, h, qt:qt + 1], accum_out=self.total[:, j, h, qt:qt + 1])
            last.then_inc(sg["exp"], 1)

    def dve_out(self, dve, n, j, recip, out):
        nc, sg, H = self.core.nc, self.sg, self.H
        dve.wait_ge(sg["exp"], H * (n + 1))
        nc.vector.reciprocal(recip, self.total[:, j, :, :]).then_inc(sg["recip"], 1)
        dve.wait_ge(sg["recip"], n + 1)
        dve.wait_ge(sg["values"], H * (n + 1))
        wait(dve, sg["o_turned"], n - 1)
        for qt in range(2):
            last = nc.vector.tensor_tensor(out[:, qt, :, :], self.ps_o[:, qt, :, :],
                                           recip[:, :, qt:qt + 1].to_broadcast([P, H, self.DH]), ALU.mult)
        last.then_inc(sg["heads_out"], 1)



def shape_constants(T):
    f32 = np.float32
    out = {}
    S, DH, H = T["L0_attn_x"].shape[1], 8, 16
    freq = np.exp(-(np.arange(0, DH, 2, dtype=f32) / f32(DH)) * np.log(f32(10000.0)))
    angle = (np.arange(S, dtype=f32)[:, None] * freq).astype(f32).astype(np.float64)
    rope = np.zeros((P, 2, 2, S), f32)
    for r in range(4):
        for d in range(DH):
            sign = -1.0 if d % 2 == 0 else 1.0
            for a, m in enumerate((DH ** -0.5, 1.0)):
                rope[32 * r + d, a, 0] = np.cos(angle[:, d // 2]) * m
                rope[32 * r + d, a, 1] = np.sin(angle[:, d // 2]) * sign * m
    out["L2_rope"] = rope

    def spread(w, swap, group):
        to = np.zeros(w.shape[:-1] + (4, P), w.dtype)
        for h in range(H):
            src = (h // 4 if group else h) * DH
            for d in range(DH):
                to[..., h // 4, 32 * (h % 4) + d] = w[..., src + (d ^ 1 if swap else d)]
        return to

    w = np.zeros((P, 2, 2, 4, P), f32)
    b = np.zeros((P, 2, 2, 4), f32)
    for a, (wn, bn) in enumerate((("L2_attn_Wq", "L2_attn_bq"), ("L2_attn_Wk", "L2_attn_bk"))):
        for s in range(2):
            w[:, a, s] = spread(T[wn], s == 1, a == 1)
            b[:, a, s] = spread(T[bn], s == 1, a == 1).T
    out["L2_w_qk"], out["L2_b_qk"] = w, b

    E = T["L2_ffn_router_w"].shape[1]
    pair = lambda w: w.reshape(w.shape[0] // 2, 2, P, -1).transpose(2, 0, 1, 3).reshape(P, w.shape[0] // 2, P)
    out["L2_w13"] = np.stack([np.concatenate([pair(T[f"L2_ffn_routed_w{k}"]), pair(T[f"L2_ffn_shared_w{k}"])], 1)
                              for k in (1, 3)], 1)
    w2 = np.concatenate([T["L2_ffn_routed_w2"], T["L2_ffn_shared_w2"]], 0)
    out["L2_w2"] = np.ascontiguousarray(w2.reshape(-1, P, P).transpose(1, 0, 2))
    out["moe_rank"] = np.broadcast_to(np.arange(E, 0, -1, dtype=f32), (P, E)).copy()
    out["moe_spread"] = np.kron(np.eye(E, dtype=f32), np.ones((1, P // 2), f32)).reshape(E, E // 2, P)
    by_tile = lambda v: v.reshape(v.shape[:-1] + (-1, P))
    out["L0_kern"] = np.ascontiguousarray(by_tile(T["L0_attn_conv_k"][:, 0]).transpose(2, 0, 1))
    out["L0_cols"] = np.stack([by_tile(T["L0_attn_" + k]) for k in ("conv_b", "b_dt", "D_ssm")]).transpose(2, 0, 1).copy()
    N2 = 2 * T["L0_attn_A_log"].shape[1]
    out["mamba_sel"] = np.repeat(np.eye(N2, dtype=f32)[:, :, None], P, axis=2)
    DIM, WIN = 64, 32
    half = np.arange(0, DIM, 2, dtype=f32)
    inv_freq = (f32(1.0) / f32(10000.0) ** (half / f32(DIM))).astype(f32)
    tok = np.arange(S, dtype=f32)
    ang = (tok[:, None] * inv_freq[None]).astype(f32).astype(np.float64)
    base = ((half + f32(0.4 * DIM)) / f32(1.4 * DIM)).astype(np.float64)
    zoom = base[None] ** ((tok - S // 2) / (WIN // 2)).astype(np.float64)[:, None]
    rope = np.zeros((S, 2, 2, DIM), np.float64)
    for a, m in enumerate((8.0 * zoom, 1.0 / zoom)):
        c, s = np.cos(ang) * m, np.sin(ang) * m
        rope[:, a, 0] = np.concatenate([c, c], 1)
        rope[:, a, 1] = np.concatenate([-s, s], 1)
    out["L1_rope"] = np.ascontiguousarray(rope.reshape(2, P, 2, 2, DIM).transpose(1, 0, 2, 3, 4)).astype(f32)
    i, c = (np.arange(P) % WIN)[:, None], np.arange(2 * WIN)[None]
    seen = (c >= i) & (c <= i + WIN)
    mask = np.where(seen, 0.0, -1e30).astype(f32)
    start = np.where(seen & ~((np.arange(P)[:, None] < WIN) & (c < WIN)), 0.0, -1e30).astype(f32)
    out["L1_mask"] = np.stack([start, mask], 1)
    out["L1_slot"] = np.kron(np.eye(2, dtype=f32), np.ones((P // 2, 1), f32))
    qs, ks = T["L1_ffn_q_scale"], T["L1_ffn_k_scale"]
    swap = lambda v: np.concatenate([v[:, DIM // 2:], v[:, :DIM // 2]], 1)
    out["L1_scales"] = np.concatenate([qs, swap(qs), ks, swap(ks)], 1)
    FF = T["L1_ffn_W2"].shape[1]
    FT = (FF + P - 1) // P
    LL = qs.shape[0]
    tiles = lambda v: np.pad(v, ((0, 0), (0, FT * P - FF))).reshape(LL, FT, P).transpose(0, 2, 1)
    w2 = np.pad(T["L1_ffn_W2"], ((0, 0), (0, FT * P - FF), (0, 0)))
    out["L1_w2"] = np.ascontiguousarray(w2.reshape(LL, FT, P, P).transpose(0, 2, 1, 3).reshape(LL, P, FT * P))
    out["L1_vecs"] = np.concatenate([np.stack([T["L1_ffn_ln_g"], T["L1_ffn_ln_b"], T["L1_ffn_b2"]], 2),
                                     tiles(T["L1_ffn_b1"][:, :FF]), tiles(T["L1_ffn_b1"][:, FF:])], 2)
    out["L3_w_oT"] = np.ascontiguousarray(T["L3_attn_w_o"].T)

    w = np.zeros((P, 2, 4, P), f32)
    b = np.zeros((P, 2, 4), f32)
    for a, (wn, bn) in enumerate((("L1_attn_Wq", "L1_attn_bq"), ("L1_attn_Wk", "L1_attn_bk"))):
        w[:, a] = spread(T[wn], False, False)
        b[:, a] = spread(T[bn], False, False).T
    out["L1_w_qk"], out["L1_b_qk"] = w, b
    out["L1_cols"] = np.stack([T["L1_attn_bo"], T["L1_attn_gn_w"].reshape(-1), T["L1_attn_gn_b"].reshape(-1)], 1)
    lvec = np.zeros((P, 4, 4, DH), f32)
    for r in range(4):
        for i, name in enumerate(("lq1", "lk1", "lq2", "lk2")):
            lvec[32 * r:32 * r + DH, i] = T["L1_attn_" + name][r::4][None]
    out["L1_lvec"] = lvec
    out["L1_gmean"] = np.kron(np.eye(H, dtype=f32), np.full((DH, DH), 1.0 / (DH * S), f32))
    return out


def stage_binary_ffn(core, T):
    nc, B, S = core.nc, core.B, core.S
    H = T["L3_ffn_w1"].shape[0]
    HT = H // P
    W = 2 * S
    with ExitStack() as ctx:
        sg = Signals(nc, ctx, "bf")

        def sb(name, shape, dt=F32):
            return ctx.enter_context(nc.sbuf_tensor("bf_" + name, shape, dt))

        def psum(name, shape, dt=F32):
            return ctx.enter_context(nc.psum_tensor("bf_" + name, shape, dt))

        ln = AdaNorm(core, ctx, sg, 3, SHIFT_B, SCALE_B)
        raw = sb("raw", [P, 2, HT, P])
        size = sb("size", [P, 2, HT, P])
        alpha = sb("alpha", [P, HT + 1])
        wT = sb("wT", [P, 2, HT, P])
        b1 = sb("b1", [P, HT])
        b2 = sb("b2", [P, 1])
        hid = sb("hid", [P, 2, HT, W])
        tmp = sb("tmp", [P, 2, W])
        ps_w = psum("ps_w", [P, 2, HT, P])
        ps_h = psum("ps_h", [P, HT, W])
        ps_o = psum("ps_o", [P, 2, W])
        ln.ps_mean, ln.ps_var = ps_w[:, :, :, :].rearrange("p a b c -> p a (b c)"), ps_o
        items = B // 2
        block = ctx.enter_context(nc.Block())

        @block.sync
        def _(sp):
            sp.dma_start(raw[:, 0, :, :], T["L3_ffn_w1"].rearrange("(t p) d -> p t d", p=P)).then_inc(sg["w_in"], 16)
            sp.dma_start(raw[:, 1, :, :].rearrange("p t c -> p (t c)"), T["L3_ffn_w2"]).then_inc(sg["w_in"], 16)
            with nc.allow_non_contiguous_dma("biases"):
                sp.dma_start(b1[:, :], T["L3_ffn_b1"].rearrange("(t p) -> p t", p=P)).then_inc(sg["b_in"], 16)
                sp.dma_start(b2[:, :], T["L3_ffn_b2"].rearrange("(p a) -> p a", a=1)).then_inc(sg["b_in"], 16)

        @block.tensor
        def _(pe):
            pe.wait_ge(sg["w_bin"], 1)
            for k in range(2):
                for t in range(HT):
                    last = pe.transpose(ps_w[:, k, t, :], raw[:, k, t, :], core.ident[:, :])
            last.then_inc(sg["w_turned"], 1)
            pe.wait_ge(sg["wT"], 1)
            ln.pe(pe)
            pe.wait_ge(sg["ln_log"], items)
            pe.wait_ge(sg["h"], items)

            def item(n, j):
                for t in range(HT):
                    if t == 0:
                        wait(pe, sg["gelu"], HT * n)
                    pe.matmul(ps_h[:, t, :], wT[:, 0, t, :], ln.h[:, bass.ds(2 * n, 2), :].rearrange("p b s -> p (b s)"),
                              start=True, stop=True).then_inc(sg["hidden"], 1)
                wait(pe, sg["biased"], n - 1)
                for t in range(HT):
                    pe.wait_ge(sg["gelu"], HT * n + t + 1)
                    last = pe.matmul(ps_o[:, j, :], wT[:, 1, t, :], hid[:, j, t, :], start=(t == 0), stop=(t == HT - 1))
                last.then_inc(sg["out"], 1)

            pairs(pe, items, item)

        @block.scalar
        def _(act):
            act.wait_ge(sg["w_in"], 32)
            for t in range(HT):
                nc.scalar.activation(size[:, 0, t, :], raw[:, 0, t, :], ACT.Abs, accum_out=alpha[:, t:t + 1])
            nc.scalar.activation(size[:, 1, :, :], raw[:, 1, :, :], ACT.Abs, accum_out=alpha[:, HT:HT + 1]).then_inc(sg["alpha"], 1)
            act.wait_ge(sg["alpha"], 1)
            nc.scalar.activation(size[:, :, :, :], raw[:, :, :, :], ACT.Sign).then_inc(sg["sign"], 1)
            ln.act(act)
            act.wait_ge(sg["b_in"], 32)

            def item(n, j):
                wait(act, sg["out"], n - 1)
                for t in range(HT):
                    act.wait_ge(sg["hidden"], HT * n + t + 1)
                    nc.scalar.activation(hid[:, j, t, :], ps_h[:, t, :], ACT.Gelu, bias=b1[:, t:t + 1]).then_inc(sg["gelu"], 1)
                act.wait_ge(sg["out"], n + 1)
                wait(act, sg["added"], n - 1)
                nc.scalar.activation(tmp[:, j, :], ps_o[:, j, :], ACT.Identity, bias=b2[:, 0:1]).then_inc(sg["biased"], 1)

            pairs(act, items, item)

        @block.vector
        def _(dve):
            dve.wait_ge(sg["alpha"], 1)
            nc.vector.tensor_scalar(alpha[:, 0:HT], alpha[:, 0:HT], 1.0 / P, None, ALU.mult)
            nc.vector.tensor_scalar(alpha[:, HT:HT + 1], alpha[:, HT:HT + 1], 1.0 / H, None, ALU.mult).then_inc(sg["bin"], 1)
            dve.wait_ge(sg["bin"], 1)
            dve.wait_ge(sg["sign"], 1)
            for t in range(HT):
                nc.vector.scalar_tensor_tensor(out=size[:, 0, t, :], in0=size[:, 0, t, :], scalar=alpha[:, t:t + 1],
                                               in1=raw[:, 0, t, :], op0=ALU.mult, op1=ALU.subtract)
            nc.vector.scalar_tensor_tensor(out=size[:, 1, :, :].rearrange("p a b -> p (a b)"),
                                           in0=size[:, 1, :, :].rearrange("p a b -> p (a b)"), scalar=alpha[:, HT:HT + 1],
                                           in1=raw[:, 1, :, :].rearrange("p a b -> p (a b)"), op0=ALU.mult,
                                           op1=ALU.subtract).then_inc(sg["bin"], 1)
            dve.wait_ge(sg["bin"], 2)
            nc.vector.tensor_tensor(raw[:, :, :, :].rearrange("p a b c -> p (a b c)"),
                                    raw[:, :, :, :].rearrange("p a b c -> p (a b c)"),
                                    size[:, :, :, :].rearrange("p a b c -> p (a b c)"), ALU.add).then_inc(sg["w_bin"], 1)
            dve.wait_ge(sg["w_turned"], 1)
            nc.vector.tensor_copy(wT[:, :, :, :], ps_w[:, :, :, :]).then_inc(sg["wT"], 1)
            ln.dve(dve)

            def item(n, j):
                dve.wait_ge(sg["biased"], n + 1)
                for k in range(2):
                    last = add_residual(core, sg, dve, n, tmp[:, j, k * S:(k + 1) * S], 2 * n + k, 3, GATE_B)
                last.then_inc(sg["added"], 1)

            pairs(dve, items, item)


class Quantizer:

    STEPS = 13

    def __init__(self, core, sb, sg, name, blocks):
        self.nc, self.sg, self.name = core.nc, sg, name
        self.amax = sb(name + "_amax", [P, blocks, 1])
        self.scale = sb(name + "_scale", [P, blocks, 1])
        self.half = sb(name + "_half", [P, blocks, 1])
        self.mag = sb(name + "_mag", [P, blocks, 16])
        self.sign = sb(name + "_sign", [P, blocks, 16])
        self.level = sb(name + "_level", [P, blocks, 16])
        self.blocks = blocks

    def act(self, act, n, src, ready):
        nc, sg, name = self.nc, self.sg, self.name
        act.wait_ge(ready, n + 1)
        wait(act, sg[name + "_done"], n)
        nc.scalar.activation(self.sign[:, :, :], src, ACT.Sign).then_inc(sg[name + "_sign"], 1)
        act.wait_ge(sg[name + "_normed"], n + 1)
        nc.scalar.activation(self.mag[:, :, :], self.mag[:, :, :], ACT.Abs).then_inc(sg[name + "_mag"], 1)

    def dve(self, dve, n, src, dst, extra=None):
        nc, sg, name, shape = self.nc, self.sg, self.name, [P, self.blocks, 16]

        def flat(t):
            return t[:, :, :].rearrange("p a b -> p (a b)")

        step = [0]

        def done(ins):
            step[0] += 1
            ins.then_inc(sg[name + "_step"], 1)
            dve.wait_ge(sg[name + "_step"], self.STEPS * n + step[0])

        done(nc.vector.tensor_reduce(self.amax[:, :, 0], src, AX.X, ALU.max, apply_absolute_value=True))
        done(nc.vector.tensor_scalar(self.scale[:, :, :], self.amax[:, :, :], 1.0 / 6.0, 1e-12, ALU.mult, ALU.max))
        done(nc.vector.reciprocal(self.amax[:, :, :], self.scale[:, :, :]))
        done(nc.vector.tensor_scalar(self.half[:, :, :], self.scale[:, :, :], 0.5, None, ALU.mult))
        nc.vector.tensor_tensor(self.mag[:, :, :], src, self.amax[:, :, :].to_broadcast(shape), ALU.mult).then_inc(sg[name + "_normed"], 1)
        dve.wait_ge(sg[name + "_mag"], n + 1)
        done(nc.vector.tensor_scalar(flat(self.level), flat(self.mag), 5.0, 2.0, ALU.is_gt, ALU.mult))
        for mid in (3.5, 2.5):
            done(nc.vector.scalar_tensor_tensor(out=flat(self.level), in0=flat(self.mag), scalar=mid, in1=flat(self.level),
                                                op0=ALU.is_gt, op1=ALU.add))
        done(nc.vector.tensor_scalar(flat(self.level), flat(self.level), 2.0, None, ALU.mult))
        for mid in (1.75, 1.25, 0.75, 0.25):
            done(nc.vector.scalar_tensor_tensor(out=flat(self.level), in0=flat(self.mag), scalar=mid, in1=flat(self.level),
                                                op0=ALU.is_gt, op1=ALU.add))
        dve.wait_ge(sg[name + "_sign"], n + 1)
        done(nc.vector.tensor_tensor(flat(self.level), flat(self.level), flat(self.sign), ALU.mult))
        if extra is not None:
            extra()
        nc.vector.tensor_tensor(dst, self.level[:, :, :], self.half[:, :, :].to_broadcast(shape), ALU.mult).then_inc(sg[name + "_done"], 1)


def stage_fp4_ffn(core, T):
    nc, B, S = core.nc, core.B, core.S
    I = T["L0_ffn_w_gate"].shape[0]
    IT = (I + P - 1) // P
    IB = I // 16
    DB = P // 16
    rows = [min(P, I - t * P) for t in range(IT)]
    with ExitStack() as ctx:
        sg = Signals(nc, ctx, "fp")

        def sb(name, shape, dt=F32):
            return ctx.enter_context(nc.sbuf_tensor("fp_" + name, shape, dt))

        def psum(name, shape, dt=F32):
            return ctx.enter_context(nc.psum_tensor("fp_" + name, shape, dt))

        ln = AdaNorm(core, ctx, sg, 0, SHIFT_B, SCALE_B)
        WB = 2 * IT * DB + IB
        qw = Quantizer(core, sb, sg, "qw", WB)
        qx = Quantizer(core, sb, sg, "qx", 2 * DB)
        qh = Quantizer(core, sb, sg, "qh", 2 * IB)
        wraw = sb("wraw", [P, WB, 16])
        wgu = sb("wgu", [P, 2, I])
        wd = sb("wd", [P, IT, P])
        h_tok = sb("h_tok", [P, 2 * DB, 16])
        hq = sb("hq", [P, 2, P])
        hqT = sb("hqT", [P, 2, P])
        gate = sb("gate", [P, 2, I])
        hid = sb("hid", [P, 2, I])
        hidq = sb("hidq", [P, 2, I])
        hidT = sb("hidT", [P, IT, S])
        h_fixed = sb("h_fixed", [P, 2, S])
        ps_a = psum("ps_a", [P, 512])
        ps_b = psum("ps_b", [P, 512])
        ps_g = psum("ps_g", [P, 2, 512])
        ps_u = psum("ps_u", [P, 2, 512])
        ps_t = psum("ps_t", [P, 512])
        ps_o = psum("ps_o", [P, 512])
        ln.ps_mean, ln.ps_var = ps_g, ps_u
        flat = "p a b -> p (a b)"
        block = ctx.enter_context(nc.Block())

        @block.sync
        def _(sp):
            sp.wait_ge(sg["w_zero"], 1)
            for k, name in enumerate(("L0_ffn_w_gate", "L0_ffn_w_up")):
                for t in range(IT):
                    c = (k * IT + t) * DB
                    sp.dma_start(wraw[0:rows[t], c:c + DB, :].rearrange(flat), T[name][t * P:t * P + rows[t], :]).then_inc(sg["w_in"], 16)
            sp.dma_start(wraw[:, 2 * IT * DB:WB, :].rearrange(flat), T["L0_ffn_w_down"]).then_inc(sg["w_in"], 16)

        @block.gpsimd
        def _(pool):
            pool.memset(wraw[:, :, :], 0.0).then_inc(sg["w_zero"], 1)
            pool.wait_ge(sg["w_in"], 16 * (2 * IT + 1))
            pool.sem_inc(sg["w_ready"], 1)

            def item(n, j):
                pool.wait_ge(sg["h"], B // 2)
                wait(pool, sg["h_turned"], n - 1)
                pool.tensor_copy(h_fixed[:, j, :], ln.h[:, bass.ds(n, 1), :].rearrange("p b s -> p (b s)")).then_inc(sg["h_fixed"], 1)

            pairs(pool, B, item)

        @block.tensor
        def _(pe):
            pe.wait_ge(sg["qw_done"], 1)
            m = 0
            for k in range(2):
                for t in range(IT):
                    wait(pe, sg["wT"], m)
                    src = wraw[:, (k * IT + t) * DB:(k * IT + t + 1) * DB, :].rearrange(flat)
                    pe.transpose(ps_a[:, 0:P], src, core.ident[:, :]).then_inc(sg["w_turned"], 1)
                    m += 1
            down = wraw[:, 2 * IT * DB:WB, :].rearrange(flat)
            for t in range(IT):
                pe.wait_ge(sg["wT"], m)
                pe.transpose(ps_a[0:rows[t], 0:P], down[:, t * P:t * P + rows[t]], core.ident[:, :]).then_inc(sg["w_turned"], 1)
                m += 1
            ln.pe(pe)
            pe.wait_ge(sg["wT"], m)
            pe.wait_ge(sg["ln_log"], B // 2)

            def front(n, j):
                pe.wait_ge(sg["h_fixed"], n + 1)
                wait(pe, sg["h_tok"], n)
                for t in range(2):
                    last = pe.transpose(ps_a[:, t * P:(t + 1) * P], h_fixed[:, j, t * P:(t + 1) * P], core.ident[:, :])
                last.then_inc(sg["h_turned"], 1)
                pe.wait_ge(sg["qx_done"], n + 1)
                wait(pe, sg["hqT"], n)
                for t in range(2):
                    last = pe.transpose(ps_b[:, t * P:(t + 1) * P], hq[:, t, :], core.ident[:, :])
                last.then_inc(sg["hq_turned"], 1)
                pe.wait_ge(sg["hqT"], n + 1)
                wait(pe, sg["silu"], n)
                wait(pe, sg["hid"], n)
                for t in range(2):
                    pe.matmul(ps_g[:, t, 0:I], hqT[:, t, :], wgu[:, 0, :], start=True, stop=True)
                    last = pe.matmul(ps_u[:, t, 0:I], hqT[:, t, :], wgu[:, 1, :], start=True, stop=True)
                last.then_inc(sg["up"], 1)

            def back(n, j):
                pe.wait_ge(sg["qh_done"], n + 1)
                for t in range(IT):
                    wait(pe, sg["hidT"], IT * n + t)
                    for k in range(2):
                        last = pe.transpose(ps_t[0:rows[t], k * P:(k + 1) * P], hidq[:, k, t * P:t * P + rows[t]], core.ident[:, :])
                    last.then_inc(sg["hid_turned"], 1)
                pe.wait_ge(sg["hidT"], IT * (n + 1))
                wait(pe, sg["added"], n)
                for t in range(IT):
                    last = pe.matmul(ps_o[:, 0:S], wd[0:rows[t], t, :], hidT[0:rows[t], t, :], start=(t == 0), stop=(t == IT - 1))
                last.then_inc(sg["out"], 1)

            def item(n, j):
                front(n, j)
                if not (isinstance(n, int) and n == 0):
                    back(n - 1, 1 - j)

            pairs(pe, B, item)
            back(B - 1, 1)

        @block.scalar
        def _(act):
            qw.act(act, 0, wraw[:, :, :], sg["w_ready"])
            ln.act(act)

            def front(n, j):
                act.wait_ge(sg["h_turned"], n + 1)
                wait(act, sg["qx_done"], n)
                act.copy(h_tok[:, :, :].rearrange(flat), ps_a[:, 0:S]).then_inc(sg["h_tok"], 1)
                qx.act(act, n, h_tok[:, :, :], sg["h_tok"])
                act.wait_ge(sg["hq_turned"], n + 1)
                wait(act, sg["up"], n)
                act.copy(hqT[:, :, :].rearrange(flat), ps_b[:, 0:S]).then_inc(sg["hqT"], 1)
                act.wait_ge(sg["up"], n + 1)
                wait(act, sg["hid"], n)
                nc.scalar.activation(gate[:, :, :], ps_g[:, :, 0:I], ACT.Silu).then_inc(sg["silu"], 1)

            def middle(n, j):
                qh.act(act, n, hid[:, :, :].rearrange("p t (a b) -> p (t a) b", b=16), sg["hid"])

            def back(n, j):
                wait(act, sg["out"], n)
                for t in range(IT):
                    act.wait_ge(sg["hid_turned"], IT * n + t + 1)
                    act.copy(hidT[0:rows[t], t, :], ps_t[0:rows[t], 0:S]).then_inc(sg["hidT"], 1)

            def item(n, j):
                front(n, j)
                if not (isinstance(n, int) and n == 0):
                    back(n - 1, 1 - j)
                middle(n, j)

            pairs(act, B, item)
            back(B - 1, 1)

        @block.vector
        def _(dve):
            dve.wait_ge(sg["w_ready"], 1)
            qw.dve(dve, 0, wraw[:, :, :], wraw[:, :, :])
            m = 0
            for k in range(2):
                for t in range(IT):
                    dve.wait_ge(sg["w_turned"], m + 1)
                    nc.vector.tensor_copy(wgu[:, k, t * P:t * P + rows[t]], ps_a[:, 0:rows[t]]).then_inc(sg["wT"], 1)
                    m += 1
            for t in range(IT):
                dve.wait_ge(sg["w_turned"], m + 1)
                nc.vector.tensor_copy(wd[0:rows[t], t, :], ps_a[0:rows[t], 0:P]).then_inc(sg["wT"], 1)
                m += 1
            ln.dve(dve)

            def item(n, j):
                dve.wait_ge(sg["h_tok"], n + 1)
                qx.dve(dve, n, h_tok[:, :, :], hq[:, :, :].rearrange("p t (a b) -> p (t a) b", b=16),
                       lambda: wait(dve, sg["hq_turned"], n))
                dve.wait_ge(sg["silu"], n + 1)
                wait(dve, sg["qh_sign"], n)
                nc.vector.tensor_tensor(hid[:, :, :], gate[:, :, :], ps_u[:, :, 0:I], ALU.mult).then_inc(sg["hid"], 1)
                if not (isinstance(n, int) and n == 0):
                    residual(n - 1)
                dve.wait_ge(sg["hid"], n + 1)
                qh.dve(dve, n, hid[:, :, :].rearrange("p t (a b) -> p (t a) b", b=16),
                       hidq[:, :, :].rearrange("p t (a b) -> p (t a) b", b=16),
                       lambda: wait(dve, sg["hid_turned"], IT * n))

            def residual(n):
                dve.wait_ge(sg["out"], n + 1)
                add_residual(core, sg, dve, n, ps_o[:, 0:S], n, 0, GATE_B).then_inc(sg["added"], 1)

            pairs(dve, B, item)
            residual(B - 1)


def stage_gqa_attention(core, T):
    nc, B, S = core.nc, core.B, core.S
    with ExitStack() as ctx:
        sg = Signals(nc, ctx, "gq")

        def sb(name, shape, dt=F32):
            return ctx.enter_context(nc.sbuf_tensor("gq_" + name, shape, dt))

        def psum(name, shape, dt=F32):
            return ctx.enter_context(nc.psum_tensor("gq_" + name, shape, dt))

        ln = AdaNorm(core, ctx, sg, 2, SHIFT_A, SCALE_A)
        hd = SmallHeads(core, ctx, sg, "gqh", True, 32)
        w = sb("w", [P, 2, 2, 4, P])
        wv = sb("wv", [P, 32])
        wo = sb("wo", [P, P])
        bias = sb("bias", [P, 2, 2, 4])
        bv = sb("bv", [P, 32])
        bo = sb("bo", [P, 1])
        rope = sb("rope", [P, 2, 2, S])
        part = sb("part", [P, 2, 2, S])
        recip = sb("recip", [P, hd.H, 2])
        o_tok = sb("o_tok", [P, 2, 2, P])
        o_feat = sb("o_feat", [P, 2, S])
        tmp = sb("tmp", [P, 2, S])
        h_fixed = sb("h_fixed", [P, 2, S])
        ps_p = psum("ps_p", [P, 2, 2, S])
        ln.ps_mean = ps_p[:, :, :, :].rearrange("p a b s -> p a (b s)")
        ln.ps_var = hd.ps_t[:, :, :, :].rearrange("p a b s -> p a (b s)")
        UNITS = 9
        block = ctx.enter_context(nc.Block())

        @block.sync
        def _(sp):
            sp.dma_start(w[:, :, :, :, :], T["L2_w_qk"]).then_inc(sg["w_in"], 16)
            sp.dma_start(wv[:, :], T["L2_attn_Wv"]).then_inc(sg["w_in"], 16)
            sp.dma_start(wo[:, :], T["L2_attn_Wo"]).then_inc(sg["w_in"], 16)
            sp.dma_start(bias[:, :, :, :], T["L2_b_qk"]).then_inc(sg["w_in"], 16)
            sp.dma_start(bv[:, :], T["L2_attn_bv"].rearrange("(a n) -> a n", a=1).to_broadcast([P, 32])).then_inc(sg["w_in"], 16)
            sp.dma_start(rope[:, :, :, :], T["L2_rope"]).then_inc(sg["w_in"], 16)
            with nc.allow_non_contiguous_dma("bias"):
                sp.dma_start(bo[:, :], T["L2_attn_bo"].rearrange("(p a) -> p a", a=1)).then_inc(sg["w_in"], 16)

        @block.gpsimd
        def _(pool):
            hd.pool_consts(pool)

            def item(n, j):
                pool.wait_ge(sg["h"], B // 2)
                wait(pool, sg["unit"], UNITS * (n - 1))
                pool.tensor_copy(h_fixed[:, j, :], ln.h[:, bass.ds(n, 1), :].rearrange("p b s -> p (b s)")).then_inc(sg["h_fixed"], 1)

            pairs(pool, B, item)

        @block.tensor
        def _(pe):
            ln.pe(pe)
            pe.wait_ge(sg["ln_log"], B // 2)
            pe.wait_ge(sg["w_in"], 16 * 7)
            pe.wait_ge(sg["mask"], 2)

            def item(n, j):
                pe.wait_ge(sg["h_fixed"], n + 1)
                for a in range(2):
                    for g in range(4):
                        u = 4 * a + g
                        wait(pe, sg["unit_read"], UNITS * n + u - 1)
                        if u == 1:
                            wait(pe, sg["biased"], n)
                        for s in range(2):
                            last = pe.matmul(ps_p[:, u % 2, s, :], w[:, a, s, g, :], h_fixed[:, j, :], start=True, stop=True)
                        last.then_inc(sg["unit"], 1)
                wait(pe, sg["unit_read"], UNITS * n + 7)
                for t in range(2):
                    last = pe.matmul(ps_p[:, 0, t, 0:32], h_fixed[:, j, t * P:(t + 1) * P], wv[:, :], start=True, stop=True)
                last.then_inc(sg["unit"], 1)
                pe.wait_ge(sg["unit_read"], UNITS * (n + 1))
                hd.pe(pe, n, j)
                pe.wait_ge(sg["heads_out"], n + 1)
                for t in range(2):
                    last = pe.transpose(ps_p[:, 1, 0, t * P:(t + 1) * P], o_tok[:, j, t, :], core.ident[:, :])
                last.then_inc(sg["o_turned"], 1)
                pe.wait_ge(sg["o_feat"], n + 1)
                pe.matmul(ps_p[:, 1, 1, :], wo[:, :], o_feat[:, j, :], start=True, stop=True).then_inc(sg["out"], 1)

            pairs(pe, B, item)

        @block.scalar
        def _(act):
            ln.act(act)

            def item(n, j):
                hd.act(act, n, j)
                act.wait_ge(sg["o_turned"], n + 1)
                wait(act, sg["out"], n - 1)
                act.copy(o_feat[:, j, :], ps_p[:, 1, 0, :]).then_inc(sg["o_feat"], 1)
                act.wait_ge(sg["out"], n + 1)
                wait(act, sg["added"], n - 1)
                nc.scalar.activation(tmp[:, j, :], ps_p[:, 1, 1, :], ACT.Identity, bias=bo[:, 0:1]).then_inc(sg["biased"], 1)

            pairs(act, B, item)

        @block.vector
        def _(dve):
            ln.dve(dve)
            dve.wait_ge(sg["w_in"], 16 * 7)

            def item(n, j):
                wait(dve, sg["scores"], hd.H * (n - 1))
                for u in range(8):
                    a, g = u // 4, u % 4
                    dve.wait_ge(sg["unit"], UNITS * n + u + 1)
                    wait(dve, sg["roped"], 8 * n + u)
                    for s in range(2):
                        last = nc.vector.scalar_tensor_tensor(out=part[:, 0, s, :], in0=ps_p[:, u % 2, s, :],
                                                              scalar=bias[:, a, s, g:g + 1], in1=rope[:, a, s, :],
                                                              op0=ALU.add, op1=ALU.mult)
                    last.then_inc(sg["unit_read"], 1)
                    dve.wait_ge(sg["unit_read"], UNITS * n + u + 1)
                    dst = (hd.q, hd.k)[a]
                    nc.vector.tensor_tensor(dst[:, j, g, :], part[:, 0, 0, :], part[:, 0, 1, :], ALU.add).then_inc(sg["roped"], 1)
                dve.wait_ge(sg["unit"], UNITS * (n + 1))
                wait(dve, sg["values"], hd.H * (n - 1))
                for t in range(2):
                    last = nc.vector.tensor_tensor(hd.v[:, j, t, :], ps_p[:, 0, t, 0:32], bv[:, :], ALU.add)
                last.then_inc(sg["unit_read"], 1)
                hd.dve(dve, n, j)
                hd.dve_out(dve, n, j, recip[:, :, :], o_tok[:, j, :, :].rearrange("p t (h d) -> p t h d", h=hd.H))
                dve.wait_ge(sg["biased"], n + 1)
                add_residual(core, sg, dve, n, tmp[:, j, :], n, 2, GATE_A).then_inc(sg["added"], 1)

            pairs(dve, B, item)


def stage_diff_attention(core, T):
    nc, B, S = core.nc, core.B, core.S
    with ExitStack() as ctx:
        sg = Signals(nc, ctx, "df")

        def sb(name, shape, dt=F32):
            return ctx.enter_context(nc.sbuf_tensor("df_" + name, shape, dt))

        def psum(name, shape, dt=F32):
            return ctx.enter_context(nc.psum_tensor("df_" + name, shape, dt))

        ln = AdaNorm(core, ctx, sg, 1, SHIFT_A, SCALE_A)
        hd = SmallHeads(core, ctx, sg, "dfh", False, P)
        w = sb("w", [P, 2, 4, P])
        wv = sb("wv", [P, P])
        wo = sb("wo", [P, P])
        bias = sb("bias", [P, 2, 4])
        bv = sb("bv", [P, P])
        col = sb("col", [P, 3])
        lvec = sb("lvec", [P, 4, 4, 8])
        lprod = sb("lprod", [P, 2, 4, 8])
        lsum = sb("lsum", [P, 2, 4])
        qscale = sb("qscale", [P, 4])
        gmean = sb("gmean", [P, P])
        recip = sb("recip", [P, hd.H, 2])
        o_tok = sb("o_tok", [P, 2, 2, P])
        o_feat = sb("o_feat", [P, 2, S])
        o_sq = sb("o_sq", [P, S])
        stat = sb("stat", [P, 2, 6])
        tmp = sb("tmp", [P, 2, S])
        h_fixed = sb("h_fixed", [P, 2, S])
        ps_p = psum("ps_p", [P, 2, 2, S])
        ln.ps_mean = ps_p[:, :, :, :].rearrange("p a b s -> p a (b s)")
        ln.ps_var = hd.ps_t[:, :, :, :].rearrange("p a b s -> p a (b s)")
        UNITS = 5
        LOADS = 8
        block = ctx.enter_context(nc.Block())

        @block.sync
        def _(sp):
            sp.dma_start(w[:, :, :, :], T["L1_w_qk"]).then_inc(sg["w_in"], 16)
            sp.dma_start(wv[:, :], T["L1_attn_Wv"]).then_inc(sg["w_in"], 16)
            sp.dma_start(wo[:, :], T["L1_attn_Wo"]).then_inc(sg["w_in"], 16)
            sp.dma_start(bias[:, :, :], T["L1_b_qk"]).then_inc(sg["w_in"], 16)
            sp.dma_start(bv[:, :], T["L1_attn_bv"].rearrange("(a n) -> a n", a=1).to_broadcast([P, P])).then_inc(sg["w_in"], 16)
            sp.dma_start(col[:, :], T["L1_cols"]).then_inc(sg["w_in"], 16)
            sp.dma_start(lvec[:, :, :, :], T["L1_lvec"]).then_inc(sg["w_in"], 16)
            sp.dma_start(gmean[:, :], T["L1_gmean"]).then_inc(sg["w_in"], 16)

        @block.gpsimd
        def _(pool):
            def item(n, j):
                pool.wait_ge(sg["h"], B // 2)
                wait(pool, sg["unit"], UNITS * (n - 1))
                pool.tensor_copy(h_fixed[:, j, :], ln.h[:, bass.ds(n, 1), :].rearrange("p b s -> p (b s)")).then_inc(sg["h_fixed"], 1)

            pairs(pool, B, item)

        @block.tensor
        def _(pe):
            ln.pe(pe)
            pe.wait_ge(sg["ln_log"], B // 2)
            pe.wait_ge(sg["w_in"], 16 * LOADS)

            def item(n, j):
                pe.wait_ge(sg["h_fixed"], n + 1)
                for u in range(4):
                    a, g = u // 2, 2 * (u % 2)
                    wait(pe, sg["unit_read"], UNITS * n + u - 1)
                    if u == 1:
                        wait(pe, sg["biased"], n)
                    for s in range(2):
                        last = pe.matmul(ps_p[:, u % 2, s, :], w[:, a, g + s, :], h_fixed[:, j, :], start=True, stop=True)
                    last.then_inc(sg["unit"], 1)
                wait(pe, sg["unit_read"], UNITS * n + 3)
                for t in range(2):
                    last = pe.matmul(ps_p[:, 0, t, 0:P], h_fixed[:, j, t * P:(t + 1) * P], wv[:, :], start=True, stop=True)
                last.then_inc(sg["unit"], 1)
                pe.wait_ge(sg["unit_read"], UNITS * (n + 1))
                hd.pe(pe, n, j)
                pe.wait_ge(sg["heads_out"], n + 1)
                for t in range(2):
                    last = pe.transpose(ps_p[:, 1, 0, t * P:(t + 1) * P], o_tok[:, j, t, :], core.ident[:, :])
                last.then_inc(sg["o_turned"], 1)
                pe.wait_ge(sg["o_feat"], n + 1)
                pe.matmul(ps_p[:, 0, 0, 0:1], gmean[:, :], stat[:, j, 0:1], start=True, stop=True).then_inc(sg["g_mean"], 1)
                pe.wait_ge(sg["o_sq"], n + 1)
                pe.matmul(ps_p[:, 0, 0, 1:2], gmean[:, :], stat[:, j, 1:2], start=True, stop=True).then_inc(sg["g_var"], 1)
                pe.wait_ge(sg["o_normed"], n + 1)
                pe.matmul(ps_p[:, 1, 1, :], wo[:, :], o_feat[:, j, :], start=True, stop=True).then_inc(sg["out"], 1)

            pairs(pe, B, item)

        @block.scalar
        def _(act):
            ln.act(act)
            act.wait_ge(sg["lsum"], 2)
            nc.scalar.activation(lsum[:, :, :], lsum[:, :, :], ACT.Exp).then_inc(sg["lexp"], 1)
            act.wait_ge(sg["w_in"], 16 * LOADS)

            def item(n, j):
                hd.act(act, n, j)
                act.wait_ge(sg["o_turned"], n + 1)
                wait(act, sg["out"], n - 1)
                nc.scalar.activation(o_feat[:, j, :], ps_p[:, 1, 0, :], ACT.Identity, accum_out=stat[:, j, 0:1]).then_inc(sg["o_feat"], 1)
                act.wait_ge(sg["o_centered"], n + 1)
                nc.scalar.activation(o_sq[:, :], o_feat[:, j, :], ACT.Square, accum_out=stat[:, j, 1:2]).then_inc(sg["o_sq"], 1)
                act.wait_ge(sg["g_var"], n + 1)
                nc.scalar.activation(stat[:, j, 3:4], ps_p[:, 0, 0, 1:2], ACT.Ln, bias=core.eps[:, 0:1]).then_inc(sg["g_log"], 1)
                act.wait_ge(sg["g_log"], n + 1)
                nc.scalar.activation(stat[:, j, 4:5], stat[:, j, 3:4], ACT.Exp, scale=-0.5).then_inc(sg["g_rstd"], 1)
                act.wait_ge(sg["out"], n + 1)
                wait(act, sg["added"], n - 1)
                nc.scalar.activation(tmp[:, j, :], ps_p[:, 1, 1, :], ACT.Identity, bias=col[:, 0:1]).then_inc(sg["biased"], 1)

            pairs(act, B, item)

        @block.vector
        def _(dve):
            dve.wait_ge(sg["w_in"], 16 * LOADS)
            for k in range(2):
                nc.vector.tensor_tensor(lprod[:, k, :, :], lvec[:, 2 * k, :, :], lvec[:, 2 * k + 1, :, :], ALU.mult).then_inc(sg["lprod"], 1)
            dve.wait_ge(sg["lprod"], 2)
            for k in range(2):
                nc.vector.tensor_reduce(lsum[:, k, :], lprod[:, k, :, :], AX.X, ALU.add).then_inc(sg["lsum"], 1)
            ln.dve(dve)
            dve.wait_ge(sg["lexp"], 1)
            nc.vector.tensor_tensor(qscale[:, :], lsum[:, 0, :], lsum[:, 1, :], ALU.subtract).then_inc(sg["qscale"], 1)
            dve.wait_ge(sg["qscale"], 1)
            nc.vector.tensor_scalar(qscale[:, :], qscale[:, :], 0.8, 8.0 ** -0.5, ALU.add, ALU.mult).then_inc(sg["qscale"], 1)
            dve.wait_ge(sg["qscale"], 2)

            def item(n, j):
                wait(dve, sg["scores"], hd.H * (n - 1))
                for u in range(4):
                    a, g = u // 2, 2 * (u % 2)
                    dve.wait_ge(sg["unit"], UNITS * n + u + 1)
                    for s in range(2):
                        if a == 0:
                            last = nc.vector.tensor_scalar(hd.q[:, j, g + s, :], ps_p[:, u % 2, s, :], bias[:, 0, g + s:g + s + 1],
                                                           qscale[:, g + s:g + s + 1], ALU.add, ALU.mult)
                        else:
                            last = nc.vector.tensor_scalar(hd.k[:, j, g + s, :], ps_p[:, u % 2, s, :], bias[:, 1, g + s:g + s + 1],
                                                           None, ALU.add)
                    last.then_inc(sg["unit_read"], 1)
                dve.wait_ge(sg["unit"], UNITS * (n + 1))
                wait(dve, sg["values"], hd.H * (n - 1))
                for t in range(2):
                    last = nc.vector.tensor_tensor(hd.v[:, j, t, :], ps_p[:, 0, t, 0:P], bv[:, :], ALU.add)
                last.then_inc(sg["unit_read"], 1)
                hd.dve(dve, n, j)
                hd.dve_out(dve, n, j, recip[:, :, :], o_tok[:, j, :, :].rearrange("p t (h d) -> p t h d", h=hd.H))
                dve.wait_ge(sg["g_mean"], n + 1)
                nc.vector.tensor_copy(stat[:, j, 2:3], ps_p[:, 0, 0, 0:1]).then_inc(sg["g_mean_copied"], 1)
                dve.wait_ge(sg["g_mean_copied"], n + 1)
                nc.vector.tensor_scalar(o_feat[:, j, :], o_feat[:, j, :], stat[:, j, 2:3], None, ALU.subtract).then_inc(sg["o_centered"], 1)
                dve.wait_ge(sg["g_rstd"], n + 1)
                nc.vector.tensor_tensor(stat[:, j, 5:6], stat[:, j, 4:5], col[:, 1:2], ALU.mult).then_inc(sg["g_scale"], 1)
                dve.wait_ge(sg["g_scale"], n + 1)
                nc.vector.tensor_scalar(o_feat[:, j, :], o_feat[:, j, :], stat[:, j, 5:6], col[:, 2:3], ALU.mult, ALU.add).then_inc(sg["o_normed"], 1)
                dve.wait_ge(sg["biased"], n + 1)
                add_residual(core, sg, dve, n, tmp[:, j, :], n, 1, GATE_A).then_inc(sg["added"], 1)

            pairs(dve, B, item)


def stage_causal_attention(core, T):
    nc, B, S = core.nc, core.B, core.S
    OT = T["L3_attn_w_q"].shape[0] // P
    INV = float(OT * P) ** -0.5
    with ExitStack() as ctx:
        sg = Signals(nc, ctx, "ca")

        def sb(name, shape, dt=F32):
            return ctx.enter_context(nc.sbuf_tensor("ca_" + name, shape, dt))

        def psum(name, shape, dt=F32):
            return ctx.enter_context(nc.psum_tensor("ca_" + name, shape, dt))

        ln = AdaNorm(core, ctx, sg, 3, SHIFT_A, SCALE_A)
        w = sb("w", [P, 4, OT, P])
        wqk = sb("wqk", [P, P])
        wov = sb("wov", [P, P])
        mask = sb("mask", [P, 3, P])
        h_tok = sb("h_tok", [P, 2, 2, P])
        q = sb("q", [P, 2, S])
        prob = sb("prob", [P, 2, 3, P])
        nmax = sb("nmax", [P, 2, 2])
        total = sb("total", [P, 2, 2])
        probT = sb("probT", [P, 2, 3, P])
        mix = sb("mix", [P, 2, S])
        h_fixed = sb("h_fixed", [P, 2, S])
        ps_m = psum("ps_m", [P, 2, 2, S])
        ps_s = psum("ps_s", [P, 2, 4, P])
        ps_t = psum("ps_t", [P, 2, 4, P])
        ps_c = psum("ps_c", [P, 2, 2, S])
        ln.ps_mean = ps_s[:, :, :, :].rearrange("p a b s -> p a (b s)")
        ln.ps_var = ps_t[:, :, :, :].rearrange("p a b s -> p a (b s)")
        block = ctx.enter_context(nc.Block())

        @block.sync
        def _(sp):
            for k, name in enumerate(("L3_attn_w_q", "L3_attn_w_k", "L3_attn_w_v")):
                sp.dma_start(w[:, k, :, :], T[name].rearrange("(t p) i -> p t i", p=P)).then_inc(sg["w_in"], 16)
            sp.dma_start(w[:, 3, :, :], T["L3_w_oT"].rearrange("(t p) i -> p t i", p=P)).then_inc(sg["w_in"], 16)

        @block.gpsimd
        def _(pool):
            pool.memset(mask[:, :, :], 0.0).then_inc(sg["mask0"], 1)
            pool.wait_ge(sg["mask0"], 1)
            for m in (0, 2):
                pool.affine_select(out=mask[:, m, :], in_=mask[:, m, :], compare_op=ALU.is_ge, fill=-1e30,
                                   base=0, pattern=[[-1, P]], channel_multiplier=1).then_inc(sg["mask"], 1)

            def item(n, j):
                pool.wait_ge(sg["h"], B // 2)
                wait(pool, sg["scores"], n - 1)
                pool.tensor_copy(h_fixed[:, j, :], ln.h[:, bass.ds(n, 1), :].rearrange("p b s -> p (b s)")).then_inc(sg["h_fixed"], 1)

            pairs(pool, B, item)

        @block.tensor
        def _(pe):
            pe.wait_ge(sg["w_in"], 64)
            for k in range(2):
                for t in range(OT):
                    last = pe.matmul(ps_m[:, k, 0, 0:P], w[:, 2 * k, t, :], w[:, 2 * k + 1, t, :], start=(t == 0), stop=(t == OT - 1))
                last.then_inc(sg["w_made"], 1)
            ln.pe(pe)
            pe.wait_ge(sg["ln_log"], B // 2)
            pe.wait_ge(sg["w_copied"], 2)

            def front(n, j):
                pe.wait_ge(sg["h_fixed"], n + 1)
                wait(pe, sg["q"], n - 1)
                wait(pe, sg["h_tok"], n - 1)
                pe.matmul(ps_m[:, j, 1, :], wqk[:, :], h_fixed[:, j, :], start=True, stop=True).then_inc(sg["queries"], 1)
                for t in range(2):
                    last = pe.transpose(ps_m[:, j, 0, t * P:(t + 1) * P], h_fixed[:, j, t * P:(t + 1) * P], core.ident[:, :])
                last.then_inc(sg["h_turned"], 1)
                pe.wait_ge(sg["q"], n + 1)
                wait(pe, sg["masked"], n - 1)
                pe.matmul(ps_s[:, j, 0, :], q[:, j, 0:P], h_fixed[:, j, 0:P], start=True, stop=True)
                pe.matmul(ps_s[:, j, 1:3, :].rearrange("p a b -> p (a b)"), q[:, j, P:2 * P], h_fixed[:, j, :],
                          start=True, stop=True).then_inc(sg["scores"], 1)

            def back(n, j):
                pe.wait_ge(sg["normed"], n + 1)
                wait(pe, sg["probT"], n - 1)
                for m in range(3):
                    last = pe.transpose(ps_t[:, j, m, :], prob[:, j, m, :], core.ident[:, :])
                last.then_inc(sg["turned"], 1)
                pe.wait_ge(sg["probT"], n + 1)
                pe.wait_ge(sg["h_tok"], n + 1)
                wait(pe, sg["added"], n - 1)
                pe.matmul(ps_c[:, j, 0, :], h_tok[:, j, 0, :], probT[:, j, 0:2, :].rearrange("p a b -> p (a b)"),
                          start=True, stop=False)
                pe.matmul(ps_c[:, j, 0, P:2 * P], h_tok[:, j, 1, :], probT[:, j, 2, :], start=False, stop=True).then_inc(sg["mixed"], 1)
                pe.wait_ge(sg["mix"], n + 1)
                pe.matmul(ps_c[:, j, 1, :], wov[:, :], mix[:, j, :], start=True, stop=True).then_inc(sg["out"], 1)

            def item(n, j):
                front(n, j)
                if not (isinstance(n, int) and n == 0):
                    back(n - 1, 1 - j)

            pairs(pe, B, item)
            back(B - 1, 1)

        @block.scalar
        def _(act):
            ln.act(act)

            def front(n, j):
                act.wait_ge(sg["queries"], n + 1)
                act.wait_ge(sg["h_turned"], n + 1)
                wait(act, sg["scores"], n - 1)
                act.copy(q[:, j, :], ps_m[:, j, 1, :]).then_inc(sg["q"], 1)
                wait(act, sg["mixed"], n - 1)
                act.copy(h_tok[:, j, :, :].rearrange("p a b -> p (a b)"), ps_m[:, j, 0, :]).then_inc(sg["h_tok"], 1)
                act.wait_ge(sg["max"], n + 1)
                nc.scalar.activation(prob[:, j, 0, :], prob[:, j, 0, :], ACT.Exp, bias=nmax[:, j, 0:1], accum_out=total[:, j, 0:1])
                nc.scalar.activation(prob[:, j, 1:3, :], prob[:, j, 1:3, :], ACT.Exp, bias=nmax[:, j, 1:2],
                                     accum_out=total[:, j, 1:2]).then_inc(sg["exp"], 1)

            def back(n, j):
                act.wait_ge(sg["turned"], n + 1)
                wait(act, sg["mixed"], n - 1)
                act.copy(probT[:, j, :, :], ps_t[:, j, 0:3, :]).then_inc(sg["probT"], 1)
                act.wait_ge(sg["mixed"], n + 1)
                wait(act, sg["out"], n - 1)
                act.copy(mix[:, j, :], ps_c[:, j, 0, :]).then_inc(sg["mix"], 1)

            def item(n, j):
                front(n, j)
                if not (isinstance(n, int) and n == 0):
                    back(n - 1, 1 - j)

            pairs(act, B, item)
            back(B - 1, 1)

        @block.vector
        def _(dve):
            for k, dst in enumerate((wqk, wov)):
                dve.wait_ge(sg["w_made"], k + 1)
                nc.vector.tensor_copy(dst[:, :], ps_m[:, k, 0, 0:P]).then_inc(sg["w_copied"], 1)
            ln.dve(dve)
            dve.wait_ge(sg["mask"], 2)

            def front(n, j):
                dve.wait_ge(sg["scores"], n + 1)
                wait(dve, sg["turned"], n - 1)
                nc.vector.scalar_tensor_tensor(out=prob[:, j, :, :].rearrange("p a b -> p (a b)"),
                                               in0=ps_s[:, j, 0:3, :].rearrange("p a b -> p (a b)"), scalar=INV,
                                               in1=mask[:, :, :].rearrange("p a b -> p (a b)"), op0=ALU.mult,
                                               op1=ALU.add).then_inc(sg["masked"], 1)
                dve.wait_ge(sg["masked"], n + 1)
                wait(dve, sg["exp"], n - 1)
                nc.vector.tensor_reduce(nmax[:, j, 0:1], prob[:, j, 0, :], AX.X, ALU.max, negate=True)
                nc.vector.tensor_reduce(nmax[:, j, 1:2], prob[:, j, 1:3, :].rearrange("p a b -> p (a b)"), AX.X, ALU.max,
                                        negate=True).then_inc(sg["max"], 1)

            def back(n, j):
                dve.wait_ge(sg["exp"], n + 1)
                nc.vector.reciprocal(total[:, j, :], total[:, j, :]).then_inc(sg["recip"], 1)
                dve.wait_ge(sg["recip"], n + 1)
                nc.vector.tensor_scalar(prob[:, j, 0, :], prob[:, j, 0, :], total[:, j, 0:1], None, ALU.mult)
                nc.vector.tensor_scalar(prob[:, j, 1:3, :].rearrange("p a b -> p (a b)"),
                                        prob[:, j, 1:3, :].rearrange("p a b -> p (a b)"), total[:, j, 1:2], None,
                                        ALU.mult).then_inc(sg["normed"], 1)
                dve.wait_ge(sg["out"], n + 1)
                add_residual(core, sg, dve, n, ps_c[:, j, 1, :], n, 3, GATE_A).then_inc(sg["added"], 1)

            def item(n, j):
                front(n, j)
                if not (isinstance(n, int) and n == 0):
                    back(n - 1, 1 - j)

            pairs(dve, B, item)
            back(B - 1, 1)


def stage_local_transformer(core, T):
    nc, B, S = core.nc, core.B, core.S
    L = T["L1_ffn_Wqkv"].shape[0]
    INNER = T["L1_ffn_Wqkv"].shape[2] // 3
    DH, WIN = 64, 32
    H = INNER // DH
    FF = T["L1_ffn_W2"].shape[1]
    FT = (FF + P - 1) // P
    frows = [min(P, FF - t * P) for t in range(FT)]
    STARTS = (0, WIN, 3 * WIN + WIN, 4 * WIN + WIN)
    with ExitStack() as ctx:
        sg = Signals(nc, ctx, "lt")

        def sb(name, shape, dt=F32):
            return ctx.enter_context(nc.sbuf_tensor("lt_" + name, shape, dt))

        def psum(name, shape, dt=F32):
            return ctx.enter_context(nc.psum_tensor("lt_" + name, shape, dt))

        prob = sb("prob", [P, 2, H, P])
        halves = prob[:, :, :, :].rearrange("p t (k h) c -> p (t k) (h c)", k=2)
        ln = AdaNorm(core, ctx, sg, 1, SHIFT_B, SCALE_B, [halves[:, k, :].rearrange("p (j w) -> p j w", j=2) for k in range(3)])
        y = ln.h
        w_qkv = sb("w_qkv", [P, 3, INNER])
        w_o = sb("w_o", [P, H // 2, P])
        w_1 = sb("w_1", [P, 2 * FF])
        w_2 = sb("w_2", [P, FT, P])
        vecs = sb("vecs", [P, 3 + 2 * FT])
        scales = sb("scales", [P, 2, 2, DH])
        rope = sb("rope", [P, 2, 2, 2, DH])
        table = sb("table", [P, 2, 2, 2, 1, DH])
        maskf = sb("maskf", [P, 2, 1, 2 * WIN])
        mask = sb("mask", [P, 2, H // 2, 2 * WIN], BF16)
        identb = sb("identb", [P, P], BF16)
        guess = sb("guess", [P, 2, H, 1])
        minus_half = sb("minus_half", [P, 2, H])
        product = sb("product", [P, H])
        three_halves = sb("three_halves", [P, H])
        xs = sb("xs", [P, 2, WIN + S])
        v = sb("v", [P, 2, 4, INNER])
        sq = sb("sq", [P, INNER])
        norm = sb("norm", [P, 2, H, 1])
        rot = sb("rot", [P, H, DH])
        qk = sb("qk", [P, 2, H, DH])
        qT = sb("qT", [P, 2, H // 2, S])
        kT = sb("kT", [P, 2, H // 2, WIN + S])
        nmax = sb("nmax", [P, 2, H, 1])
        esc = sb("esc", [P, 2, H, 1, 2 * WIN])
        total = sb("total", [P, 2, H, 1])
        share = sb("share", [P, 2, H, 2, 1])
        slot = sb("slot", [P, 1, 2])
        probT = sb("probT", [P, 2, H // 2, P])
        att = sb("att", [P, H // 2, S])
        xs2 = sb("xs2", [P, S])
        cen = sb("cen", [P, S])
        csq = sb("csq", [P, S])
        rstd = sb("rstd", [P, 4, S])
        half_eps = sb("half_eps", [P, 1])
        xn = sb("xn", [P, S])
        gel = sb("gel", [P, FT, S])
        hid = sb("hid", [P, FT, S])
        A = psum("A", [P, 2, 2 * 512])
        Bp = psum("B", [P, 2, 2 * 512])
        ln.ps_mean = A[:, :, 0:2 * S]
        ln.ps_var = Bp[:, :, 0:2 * S]
        FRONT, BACK = 2, 4
        NEWTON = 3
        ROOT = 4 * NEWTON
        block = ctx.enter_context(nc.Block())

        ORDER = ("V0", "V1", "sum0", "V2", "sum1", "V3", "q0", "PT00", "PT01", "O0", "k0", "PT10", "PT11", "O1", "q1", "Tq0",
                 "Wo", "Tk0", "mean", "k1", "var", "Tq1", "S0", "xn", "Tk1", "gate", "ffn", "S1")
        FRONT_STEPS = ("V0", "V1", "V2", "V3", "q0", "k0", "q1", "k1", "Tq0", "Tk0", "Tq1", "Tk1", "S0", "S1")

        class Item:
            def __init__(self, l, b, j):
                self.n, self.l, self.b, self.j = B * l + b, l, b, j

        def run(eng, steps, layer_start):
            def body(back, front):
                for name in ORDER:
                    item, other = (front, back) if name in FRONT_STEPS else (back, front)
                    if item is not None and name in steps:
                        steps[name](item, other)

            def layer(l):
                layer_start(l)
                body(None, Item(l, 0, 0))

                def pair(b):
                    body(Item(l, b, 0), Item(l, b + 1, 1))
                    body(Item(l, b + 1, 1), Item(l, b + 2, 0))

                if isinstance(l, int):
                    pair(0)
                    if B > 4:
                        with eng.Fori(1, B // 2 - 1) as i:
                            pair(2 * i)
                else:
                    with eng.Fori(0, B // 2 - 1) as i:
                        pair(2 * i)
                body(Item(l, B - 2, 0), Item(l, B - 1, 1))
                body(Item(l, B - 1, 1), None)

            layer(0)
            with eng.Fori(1, L) as l:
                layer(l)

        def first(item):
            return isinstance(item.n, int) and item.n == 0

        @block.sync
        def _(sp):
            sp.dma_start(rope[:, :, :, :, :], T["L1_rope"]).then_inc(sg["c_in"], 16)
            sp.dma_start(maskf[:, :, 0, :], T["L1_mask"]).then_inc(sg["c_in"], 16)
            sp.dma_start(slot[:, 0, :], T["L1_slot"]).then_inc(sg["c_in"], 16)

            sp.wait_ge(sg["h"], B // 2)
            sp.wait_ge(sg["zeros"], 8)

            def weights(l):
                one = bass.ds(l, 1)
                wait(sp, sg["qk_proj"], 4 * B * l)
                sp.wait_ge(sg["zeros"], 8)
                wait(sp, sg["table"], l)
                sp.wait_ge(sg["zeros"], 8)
                sp.dma_start(w_qkv[:, :, :].rearrange("p a n -> p (a n)"), T["L1_ffn_Wqkv"][one, :, :].rearrange("l p n -> p (l n)")).then_inc(sg["front_in"], 16)
                sp.dma_start(scales[:, :, :, :].rearrange("p a b d -> p (a b d)"),
                             T["L1_scales"][one, :].to_broadcast([P, 4 * DH])).then_inc(sg["front_in"], 16)
                wait(sp, sg["y_ffn"], B * l)
                sp.wait_ge(sg["zeros"], 8)
                sp.dma_start(w_o[:, :, :], T["L1_ffn_Wo"][one, :, :].rearrange("l (t p) n -> p (l t) n", p=P)).then_inc(sg["back_in"], 16)
                sp.dma_start(w_1[:, :], T["L1_ffn_W1"][one, :, :].rearrange("l p n -> p (l n)")).then_inc(sg["back_in"], 16)
                sp.dma_start(w_2[:, :, :].rearrange("p a n -> p (a n)"), T["L1_w2"][one, :, :].rearrange("l p n -> p (l n)")).then_inc(sg["back_in"], 16)
                sp.dma_start(vecs[:, :], T["L1_vecs"][one, :, :].rearrange("l p n -> p (l n)")).then_inc(sg["back_in"], 16)

            def tokens(m, other):
                wait(sp, sg["qk_proj"], 4 * (m.n - 1))
                sp.wait_ge(sg["zeros"], 8)
                sp.dma_start(xs[0:64, m.j, WIN:], y[0:64, bass.ds(m.b, 1), :].rearrange("p b s -> p (b s)")).then_inc(sg[f"xs{m.j}"], 16)
                sp.dma_start(xs[64:P, m.j, WIN + 1:], y[64:P, bass.ds(m.b, 1), 0:S - 1].rearrange("p b s -> p (b s)")).then_inc(sg[f"xs{m.j}"], 16)

            run(sp, {"V0": tokens}, weights)

        @block.gpsimd
        def _(pool):
            pool.memset(half_eps[:, :], -LN_EPS / 2).then_inc(sg["zeros"], 1)
            pool.memset(three_halves[:, :], 1.5).then_inc(sg["zeros"], 1)
            pool.memset(xs[:, :, :], 0.0).then_inc(sg["zeros"], 1)
            pool.memset(xs2[:, :], 0.0).then_inc(sg["zeros"], 1)
            pool.memset(kT[:, :, :, :], 0.0).then_inc(sg["zeros"], 1)
            pool.wait_ge(sg["c_in"], 48)
            pool.tensor_copy(identb[:, :], core.ident[:, :]).then_inc(sg["zeros"], 1)
            for t in range(2):
                pool.tensor_copy(mask[:, t, :, :], maskf[:, t, :, :].to_broadcast([P, H // 2, 2 * WIN])).then_inc(sg["zeros"], 1)
            def inverse_norm(u):
                def step(m, other):
                    n, done = 4 * m.n + u, 0
                    y, x = guess[:, u % 2, :, 0], minus_half[:, u % 2, :]
                    pool.wait_ge(sg["seed"], n + 1)
                    for i in range(NEWTON):
                        for out, a, b, op in ((product, y, y, ALU.mult), (product, product[:, :], x, ALU.mult),
                                              (product, product[:, :], three_halves[:, :], ALU.add), (None, product[:, :], y, ALU.mult)):
                            pool.tensor_tensor(y if out is None else out[:, :], a, b, op).then_inc(sg["root"], 1)
                            done += 1
                            pool.wait_ge(sg["root"], ROOT * n + done)
                    pool.wait_ge(sg["rotated"], n + 1)
                    pool.tensor_tensor(qk[:, u % 2, :, :], qk[:, u % 2, :, :], guess[:, u % 2, :, :].to_broadcast([P, H, DH]),
                                       ALU.mult).then_inc(sg["qk"], 1)
                return step

            def normalize(t):
                def step(n, other):
                    pool.wait_ge(sg["recip"], 2 * n.n + t + 1)
                    wait(pool, sg["p_turned"], 4 * n.n - 2 + 2 * t)
                    pool.tensor_tensor(prob[:, t, :, :].rearrange("p h (s c) -> p h s c", s=2),
                                       esc[:, t, :, :, :].to_broadcast([P, H, 2, 2 * WIN]),
                                       share[:, t, :, :, :].to_broadcast([P, H, 2, 2 * WIN]), ALU.mult).then_inc(sg["prob"], 1)
                return step

            steps = {"sum0": normalize(0), "sum1": normalize(1), "q0": inverse_norm(0), "k0": inverse_norm(1),
                     "q1": inverse_norm(2), "k1": inverse_norm(3)}
            run(pool, steps, lambda l: None)

        @block.tensor
        def _(pe):
            ln.pe(pe)
            pe.wait_ge(sg["ln_log"], B // 2)
            pe.wait_ge(sg["zeros"], 8)

            def values(i):
                def step(m, other):
                    if i == 0:
                        pe.wait_ge(sg[f"xs{m.j}"], 16 * (m.n - m.j) + 32)
                    if i < 2:
                        wait(pe, sg["ffn_h" if i else "gelu"], m.n if other is None else m.n - 1)
                    if i < 2 and other is not None:
                        pe.wait_ge(sg["s_read"], 2 * other.n + i + 1)
                    if i >= 2:
                        pe.wait_ge(sg["v"], 4 * m.n + i - 1)
                    c = STARTS[i]
                    for k in range(2):
                        last = pe.matmul(A[:, i % 2, 512 * k:512 * k + 512], xs[:, m.j, c:c + P],
                                         w_qkv[:, 2, 512 * k:512 * k + 512], start=True, stop=True)
                    last.then_inc(sg["v_proj"], 1)
                return step

            def project(u):
                a, t = u % 2, u // 2
                buf = 1 if u == 3 else 0

                def step(m, other):
                    if u == 0:
                        pe.wait_ge(sg["v"], 4 * m.n + 3)
                    elif u == 3:
                        if other is None:
                            pe.wait_ge(sg["v"], 4 * m.n + 4)
                        else:
                            pe.wait_ge(sg["o_read"], 2 * other.n + 2)
                    else:
                        pe.wait_ge(sg["qk_read"], 4 * m.n + u)
                    c = WIN + P * t
                    for k in range(2):
                        last = pe.matmul(A[:, buf, 512 * k:512 * k + 512], xs[:, m.j, c:c + P],
                                         w_qkv[:, a, 512 * k:512 * k + 512], start=True, stop=True)
                    last.then_inc(sg["qk_proj"], 1)
                return step

            def turn_qk(u):
                def step(m, other):
                    pe.wait_ge(sg["qk"], 4 * m.n + u + 1)
                    if u == 0:
                        if other is None:
                            wait(pe, sg["pT"], 4 * m.n)
                        else:
                            pe.wait_ge(sg["pT"], 4 * other.n + 3)
                    wait(pe, sg["qkT"], 4 * m.n + u)
                    for g in range(H // 2):
                        last = pe.transpose(Bp[:, 0, P * g:P * g + P],
                                            qk[:, u % 2, 2 * g:2 * g + 2, :].rearrange("p a b -> p (a b)"), core.ident[:, :])
                    last.then_inc(sg["qk_turned"], 1)
                return step

            def scores(t):
                def step(n, other):
                    pe.wait_ge(sg["qkT"], 4 * n.n + 2 * t + 2)
                    pe.wait_ge(sg["qk_read"], 4 * n.n + 3 + t)
                    if t == 1 and other is not None:
                        pe.wait_ge(sg["ffn_h"], other.n + 1)
                    for k in range(2):
                        pe.matmul(A[:, t, 512 * k:512 * k + 512], identb[:, :], mask[:, t, :, :].rearrange("p h c -> p (h c)"),
                                  start=True, stop=False, skip_group_check=True)
                    for g in range(H // 2):
                        for w in range(4):
                            for k in range(2):
                                r, c = 64 * k, P * t + WIN * w
                                last = pe.matmul(A[WIN * w:WIN * w + WIN, t, 512 * k + 64 * g:512 * k + 64 * g + 64],
                                                 qT[r:r + 64, n.j, g, c:c + WIN], kT[r:r + 64, n.j, g, c:c + 2 * WIN],
                                                 start=False, stop=(g == H // 2 - 1), skip_group_check=True,
                                                 tile_position=(r, WIN * w))
                    last.then_inc(sg["scores"], 1)
                return step

            def turn_p(t, k):
                def step(n, other):
                    i = 2 * t + k
                    pe.wait_ge(sg["prob"], 2 * n.n + t + 1)
                    if i == 0:
                        pe.wait_ge(sg["qkT"], 4 * n.n + 4)
                    elif i == 1:
                        wait(pe, sg["y_ffn"], n.n)
                    else:
                        pe.wait_ge(sg["pT"], 4 * n.n + i - 1)
                    for h in range(8):
                        last = pe.transpose(Bp[:, k, P * h:P * h + P], prob[:, t, 8 * k + h, :], core.ident[:, :])
                    last.then_inc(sg["p_turned"], 1)
                return step

            def outputs(t):
                def step(n, other):
                    pe.wait_ge(sg["pT"], 4 * n.n + 2 * t + 2)
                    if t == 1:
                        pe.wait_ge(sg["o_read"], 2 * n.n + 1)
                    elif other is not None:
                        pe.wait_ge(sg["v"], 4 * other.n + 4)
                    else:
                        pe.wait_ge(sg["s_read"], 2 * n.n + 2)
                        pe.wait_ge(sg["ffn_h"], n.n)
                    for h in range(H):
                        r = 64 * (h % 2)
                        for e in range(2):
                            rhs = probT[:, h % 2, h // 2, :].rearrange("p (a b c) -> p a b c", a=2, b=2)[:, :, e, :]
                            out = A[r:r + 64, 1, P * (h // 2):P * (h // 2) + P].rearrange("p (a b c) -> p a b c", a=2, b=2)[:, :, e, :]
                            last = pe.matmul(out, v[:, n.j, 2 * t + e, DH * h:DH * h + DH], rhs, start=True, stop=True,
                                             tile_position=(0, r))
                    last.then_inc(sg["o_made"], 1)
                return step

            def project_out(n, other):
                pe.wait_ge(sg["o_read"], 2 * n.n + 2)
                pe.wait_ge(sg["pT"], 4 * n.n + 4)
                for g in range(H // 2):
                    last = pe.matmul(Bp[:, 1, 0:S], w_o[:, g, :], att[:, g, :], start=(g == 0), stop=(g == H // 2 - 1))
                last.then_inc(sg["attn_out"], 1)

            def mean(n, other):
                pe.wait_ge(sg["xs2"], n.n + 1)
                pe.matmul(Bp[:, 1, 0:S], core.mean_w[:, :], xs2[:, :], start=True, stop=True).then_inc(sg["f_mean"], 1)

            def var(n, other):
                pe.wait_ge(sg["f_square"], n.n + 1)
                pe.matmul(Bp[:, 1, 0:S], core.mean_w[:, :], csq[:, :], start=True, stop=True).then_inc(sg["f_sumsq"], 1)

            def gate(n, other):
                pe.wait_ge(sg["xn"], n.n + 1)
                if other is not None:
                    pe.wait_ge(sg["s_read"], 2 * other.n + 1)
                    pe.wait_ge(sg["qk_read"], 4 * other.n + 4)
                for k in range(2):
                    for t in range(FT):
                        c = FF * (1 - k) + P * t
                        last = pe.matmul(A[0:frows[t], k, S * t:S * t + S], w_1[:, c:c + frows[t]], xn[:, :], start=True, stop=True)
                    last.then_inc(sg["f_up"], 1)

            def ffn(n, other):
                pe.wait_ge(sg["ffn_h"], n.n + 1)
                pe.wait_ge(sg["f_var"], n.n + 1)
                for t in range(FT):
                    last = pe.matmul(Bp[:, 1, 0:S], w_2[0:frows[t], t, :], hid[0:frows[t], t, :], start=(t == 0), stop=(t == FT - 1))
                last.then_inc(sg["f_down"], 1)

            steps = {"S0": scores(0), "S1": scores(1), "O0": outputs(0), "O1": outputs(1), "Wo": project_out, "mean": mean,
                     "var": var, "gate": gate, "ffn": ffn}
            steps.update({f"V{i}": values(i) for i in range(4)})
            steps.update({f"PT{t}{k}": turn_p(t, k) for t in range(2) for k in range(2)})
            for u, name in enumerate(("q0", "k0", "q1", "k1")):
                steps[name], steps["T" + name] = project(u), turn_qk(u)

            def start(l):
                pe.wait_ge(sg["front_in"], 16 * FRONT * (l + 1))
                pe.wait_ge(sg["back_in"], 16 * BACK * (l + 1))

            run(pe, steps, start)

        @block.scalar
        def _(act):
            ln.act(act)
            act.wait_ge(sg["zeros"], 8)

            def values(i):
                def step(m, other):
                    act.wait_ge(sg["v_proj"], 4 * m.n + i + 1)
                    wait(act, sg["o_made"], 2 * (m.n - 1))
                    act.copy(v[:, m.j, i, :], A[:, i % 2, :]).then_inc(sg["v"], 1)
                return step

            def square(u):
                def step(m, other):
                    act.wait_ge(sg["qk_proj"], 4 * m.n + u + 1)
                    wait(act, sg["sumsq"], 4 * m.n + u)
                    nc.scalar.activation(sq[:, :], A[:, 1 if u == 3 else 0, :], ACT.Square).then_inc(sg["square"], 1)
                return step

            def turned_qk(u):
                a, t = u % 2, u // 2

                def step(m, other):
                    act.wait_ge(sg["qk_turned"], 4 * m.n + u + 1)
                    wait(act, sg["scores"], 2 * (m.n - 1))
                    src = Bp[:, 0, :].rearrange("p (g s) -> p g s", s=P)
                    dst = kT[:, m.j, :, WIN + P * t:WIN + P * t + P] if a else qT[:, m.j, :, P * t:P * t + P]
                    act.copy(dst, src).then_inc(sg["qkT"], 1)
                return step

            def exps(t):
                def step(n, other):
                    act.wait_ge(sg["s_read"], 2 * n.n + t + 1)
                    nc.scalar.activation(esc[:, t, :, 0, :], esc[:, t, :, 0, :], ACT.Exp).then_inc(sg["exp"], 1)
                return step

            def turned_p(t, k):
                def step(n, other):
                    i = 2 * t + k
                    act.wait_ge(sg["p_turned"], 4 * n.n + i + 1)
                    wait(act, sg["o_made"], 2 * n.n + t)
                    act.copy(probT[:, k, :, :].rearrange("p h q -> p (h q)"), Bp[:, k, :]).then_inc(sg["pT"], 1)
                return step

            def outputs(t):
                def step(n, other):
                    act.wait_ge(sg["o_made"], 2 * n.n + t + 1)
                    wait(act, sg["attn_out"], n.n)
                    act.copy(att[:, :, P * t:P * t + P], A[:, 1, :].rearrange("p (g s) -> p g s", s=P)).then_inc(sg["o_read"], 1)
                return step

            def ffn_tokens(n, other):
                yb = y[:, bass.ds(n.b, 1), :].rearrange("p b s -> p (b s)")
                act.wait_ge(sg["y_attn"], n.n + 1)
                act.copy(xs2[0:64, :], yb[0:64, :])
                act.copy(xs2[64:P, 1:S], yb[64:P, 0:S - 1]).then_inc(sg["xs2"], 1)

            def ffn_square(n, other):
                act.wait_ge(sg["f_centered"], n.n + 1)
                wait(act, sg["f_sumsq"], n.n)
                nc.scalar.activation(csq[:, :], cen[:, :], ACT.Square).then_inc(sg["f_square"], 1)

            def ffn_var(n, other):
                act.wait_ge(sg["f_sumsq"], n.n + 1)
                wait(act, sg["xn0"], n.n)
                nc.scalar.activation(rstd[:, 0, :], Bp[:, 1, 0:S], ACT.Identity, bias=core.eps[:, 0:1])
                nc.scalar.activation(rstd[:, 1, :], Bp[:, 1, 0:S], ACT.Identity, bias=half_eps[:, 0:1], scale=-0.5).then_inc(sg["f_var"], 1)

            def gelu(n, other):
                act.wait_ge(sg["f_up"], 2 * n.n + 1)
                wait(act, sg["ffn_h"], n.n)
                for t in range(FT):
                    last = nc.scalar.activation(gel[0:frows[t], t, :], A[0:frows[t], 0, S * t:S * t + S], ACT.Gelu,
                                                bias=vecs[0:frows[t], 3 + FT + t:4 + FT + t])
                last.then_inc(sg["gelu"], 1)

            steps = {"S0": exps(0), "S1": exps(1), "O0": outputs(0), "O1": outputs(1), "Wo": ffn_tokens, "mean": ffn_square, "var": ffn_var, "gate": gelu}
            steps.update({f"V{i}": values(i) for i in range(4)})
            steps.update({f"PT{t}{k}": turned_p(t, k) for t in range(2) for k in range(2)})
            for u, name in enumerate(("q0", "k0", "q1", "k1")):
                steps[name], steps["T" + name] = square(u), turned_qk(u)
            run(act, steps, lambda l: act.wait_ge(sg["back_in"], 16 * BACK * (l + 1)))

        @block.vector
        def _(dve):
            ln.dve(dve)
            dve.wait_ge(sg["c_in"], 48)

            def start(l):
                dve.wait_ge(sg["front_in"], 16 * FRONT * (l + 1))
                dve.wait_ge(sg["back_in"], 16 * BACK * (l + 1))
                for t in range(2):
                    last = nc.vector.tensor_tensor(table[:, t, :, :, 0, :].rearrange("p a b d -> p (a b d)"),
                                                   rope[:, t, :, :, :].rearrange("p a b d -> p (a b d)"),
                                                   scales[:, :, :, :].rearrange("p a b d -> p (a b d)"), ALU.mult)
                last.then_inc(sg["table"], 1)
                dve.wait_ge(sg["table"], l + 1)

            def rotate(u):
                a, t = u % 2, u // 2

                def step(m, other):
                    n = 4 * m.n + u
                    src = A[:, 1 if u == 3 else 0, :].rearrange("p (h d) -> p h d", h=H)
                    dve.wait_ge(sg["square"], n + 1)
                    wait(dve, sg["qk"], n - 1)
                    nc.vector.tensor_reduce(norm[:, u % 2, :, 0], sq[:, :].rearrange("p (h d) -> p h d", h=H), AX.X, ALU.add).then_inc(sg["sumsq"], 1)
                    wait(dve, sg["qk_turned"], n - 1)
                    wait(dve, sg["rotated"], n)
                    nc.vector.tensor_tensor(qk[:, u % 2, :, :], src, table[:, t, a, 0, :, :].to_broadcast([P, H, DH]), ALU.mult)
                    HD = DH // 2

                    def half(k):
                        return nc.vector.tensor_tensor(rot[:, :, HD * k:HD * k + HD], src[:, :, HD * (1 - k):HD * (1 - k) + HD],
                                                       table[:, t, a, 1, :, HD * k:HD * k + HD].to_broadcast([P, H, HD]), ALU.mult)

                    x, y = norm[:, u % 2, :, 0], guess[:, u % 2, :, 0].bitcast(I32)
                    dve.wait_ge(sg["sumsq"], n + 1)
                    nc.vector.tensor_scalar(x, x, 1e-24, None, ALU.max).then_inc(sg["floor"], 1)
                    half(0)
                    dve.wait_ge(sg["floor"], n + 1)
                    nc.vector.tensor_scalar(y, x.bitcast(I32), 1, -1, ALU.logical_shift_right, ALU.bitwise_xor).then_inc(sg["shifted"], 1)
                    nc.vector.tensor_scalar(minus_half[:, u % 2, :], x, -0.5, None, ALU.mult)
                    half(1).then_inc(sg["qk_read"], 1)
                    dve.wait_ge(sg["shifted"], n + 1)
                    nc.vector.tensor_scalar(y, y, float(0x5f3759df + 1), None, ALU.add).then_inc(sg["seed"], 1)
                    dve.wait_ge(sg["qk_read"], n + 1)
                    nc.vector.tensor_tensor(qk[:, u % 2, :, :], qk[:, u % 2, :, :], rot[:, :, :], ALU.add).then_inc(sg["rotated"], 1)
                return step

            def softmax(t):
                def step(n, other):
                    dve.wait_ge(sg["scores"], 2 * n.n + t + 1)
                    s = A[:, t, :].rearrange("p (h c) -> p h c", h=H)
                    nc.vector.tensor_reduce(nmax[:, t, :, 0], s, AX.X, ALU.max).then_inc(sg["max"], 1)
                    dve.wait_ge(sg["max"], 2 * n.n + t + 1)
                    wait(dve, sg["prob"], 2 * n.n - 1 + t)
                    nc.vector.tensor_tensor(esc[:, t, :, 0, :], s, nmax[:, t, :, :].to_broadcast([P, H, 2 * WIN]), ALU.subtract).then_inc(sg["s_read"], 1)
                return step

            def sums(t):
                def step(n, other):
                    dve.wait_ge(sg["exp"], 2 * n.n + t + 1)
                    nc.vector.tensor_reduce(total[:, t, :, 0], esc[:, t, :, 0, :], AX.X, ALU.add).then_inc(sg["sum"], 1)
                    dve.wait_ge(sg["sum"], 2 * n.n + t + 1)
                    nc.vector.reciprocal(total[:, t, :, :], total[:, t, :, :]).then_inc(sg["inverse"], 1)
                    dve.wait_ge(sg["inverse"], 2 * n.n + t + 1)
                    nc.vector.tensor_tensor(share[:, t, :, :, 0], total[:, t, :, :].to_broadcast([P, H, 2]),
                                            slot[:, :, :].to_broadcast([P, H, 2]), ALU.mult).then_inc(sg["recip"], 1)
                return step

            def y_of(n):
                return y[:, bass.ds(n.b, 1), :].rearrange("p b s -> p (b s)")

            def attended(n, other):
                dve.wait_ge(sg["attn_out"], n.n + 1)
                nc.vector.tensor_tensor(y_of(n), y_of(n), Bp[:, 1, 0:S], ALU.add).then_inc(sg["y_attn"], 1)

            def center(n, other):
                dve.wait_ge(sg["f_mean"], n.n + 1)
                nc.vector.tensor_tensor(cen[:, :], xs2[:, :], Bp[:, 1, 0:S], ALU.subtract).then_inc(sg["f_centered"], 1)

            def normed(n, other):
                dve.wait_ge(sg["f_var"], n.n + 1)
                x, minus_half_x, y, yy = (rstd[:, i, :] for i in range(4))
                F_ROOT, done = 1 + 3 * NEWTON, 0

                def then(instruction):
                    nonlocal done
                    done += 1
                    instruction.then_inc(sg["f_root"], 1)
                    dve.wait_ge(sg["f_root"], F_ROOT * n.n + done)

                nc.vector.tensor_scalar(y.bitcast(I32), x.bitcast(I32), 1, -1, ALU.logical_shift_right, ALU.bitwise_xor).then_inc(sg["f_shifted"], 1)
                dve.wait_ge(sg["f_shifted"], n.n + 1)
                then(nc.vector.tensor_scalar(y.bitcast(I32), y.bitcast(I32), float(0x5f3759df + 1), None, ALU.add))
                for i in range(NEWTON):
                    then(nc.vector.tensor_tensor(yy, y, y, ALU.mult))
                    then(nc.vector.tensor_tensor(yy, yy, minus_half_x, ALU.mult))
                    then(nc.vector.scalar_tensor_tensor(out=y, in0=yy, scalar=1.5, in1=y, op0=ALU.add, op1=ALU.mult))
                wait(dve, sg["f_up"], 2 * n.n)
                nc.vector.tensor_tensor(xn[:, :], cen[:, :], y, ALU.mult).then_inc(sg["xn0"], 1)
                dve.wait_ge(sg["xn0"], n.n + 1)
                nc.vector.tensor_scalar(xn[:, :], xn[:, :], vecs[:, 0:1], vecs[:, 1:2], ALU.mult, ALU.add).then_inc(sg["xn"], 1)

            def hidden(n, other):
                dve.wait_ge(sg["gelu"], n.n + 1)
                dve.wait_ge(sg["f_up"], 2 * n.n + 2)
                wait(dve, sg["f_down"], n.n)
                for t in range(FT):
                    r = frows[t]
                    last = nc.vector.scalar_tensor_tensor(out=hid[0:r, t, :], in0=A[0:r, 1, S * t:S * t + S], scalar=vecs[0:r, 3 + t:4 + t],
                                                          in1=gel[0:r, t, :], op0=ALU.add, op1=ALU.mult)
                last.then_inc(sg["ffn_h"], 1)

            def ffn_out(n, other):
                dve.wait_ge(sg["f_down"], n.n + 1)
                nc.vector.scalar_tensor_tensor(out=y_of(n), in0=Bp[:, 1, 0:S], scalar=vecs[:, 2:3], in1=y_of(n), op0=ALU.add,
                                               op1=ALU.add).then_inc(sg["y_ffn"], 1)

            steps = {"S0": softmax(0), "S1": softmax(1), "sum0": sums(0), "sum1": sums(1), "q0": rotate(0), "k0": rotate(1),
                     "q1": rotate(2), "k1": rotate(3), "Wo": attended, "mean": center, "xn": normed, "gate": hidden, "ffn": ffn_out}
            run(dve, steps, start)
            dve.wait_ge(sg["y_ffn"], B * L)
            for b in range(B):
                add_residual(core, sg, dve, b, y[:, b, :], b, 1, GATE_B)


def stage_mamba(core, T):
    nc, B, S = core.nc, core.B, core.S
    C2 = T["L0_attn_conv_b"].shape[0]
    CT = C2 // P
    R = T["L0_attn_W_dt"].shape[0]
    N = T["L0_attn_A_log"].shape[1]
    TAPS = T["L0_attn_conv_k"].shape[0]
    G = N // 2
    assert CT == 2
    with ExitStack() as ctx:
        sg = Signals(nc, ctx, "mb")

        def sb(name, shape, dt=F32):
            return ctx.enter_context(nc.sbuf_tensor("mb_" + name, shape, dt))

        def psum(name, shape, dt=F32):
            return ctx.enter_context(nc.psum_tensor("mb_" + name, shape, dt))

        ln = AdaNorm(core, ctx, sg, 0, SHIFT_A, SCALE_A)
        w_in = sb("w_in", [P, 4, P])
        w_xp = sb("w_xp", [P, CT, R + 2 * N])
        w_dt = sb("w_dt", [R, CT, P])
        w_out = sb("w_out", [P, CT, P])
        b_in = sb("b_in", [P, 4])
        kern = sb("kern", [P, TAPS, CT])
        cols = sb("cols", [P, 3, CT])
        b_out = sb("b_out", [P, 1])
        b_r = sb("b_r", [R, 1])
        b_n = sb("b_n", [2 * N, 1])
        A = sb("A", [P, CT, N])
        sel = sb("sel", [2 * N, 2 * N, P])
        one = sb("one", [P, 1])
        xpad = sb("xpad", [P, CT, TAPS - 1 + S])
        cz = sb("cz", [P, 2, 4, S])
        sg4 = sb("sg4", [P, 4, S])
        dti = sb("dti", [R, S])
        bc = sb("bc", [2 * N, 2, S])
        soft = sb("soft", [P, CT, S])
        dt = sb("dt", [P, 2, CT, S])
        u = sb("u", [P, 2, CT, 1, S])
        decay = sb("decay", [P, 2, CT, 2, S])
        drive = sb("drive", [P, 2, CT, 2, S])
        state = sb("state", [P, CT, 2, S])
        read = sb("read", [P, 2, CT, 2, S])
        y = sb("y", [P, 2, CT, S])
        tmp = sb("tmp", [P, 2, S])
        ps_a = psum("ps_a", [P, CT, S])
        ps_z = psum("ps_z", [P, CT, S])
        ps_c = psum("ps_c", [P, 2, S])
        ps_b = psum("ps_b", [P, 2, 1, 2, S])
        ps_n = psum("ps_n", [P, 2, 1, 2, S])
        ps_y = psum("ps_y", [P, CT * S])
        ln.ps_mean = ps_b[:, :, 0, :, :].rearrange("p j k s -> p j (k s)")
        ln.ps_var = ps_n[:, :, 0, :, :].rearrange("p j k s -> p j (k s)")
        LOADS = 12
        flat = "p a b -> p (a b)"
        block = ctx.enter_context(nc.Block())

        @block.sync
        def _(sp):
            sp.dma_start(w_in[:, :, :], T["L0_attn_W_in"].rearrange("p (t m) -> p t m", m=P)).then_inc(sg["w_in"], 16)
            sp.dma_start(w_xp[:, :, :], T["L0_attn_W_xp"].rearrange("(t p) m -> p t m", p=P)).then_inc(sg["w_in"], 16)
            sp.dma_start(w_dt[:, :, :], T["L0_attn_W_dt"].rearrange("p (t m) -> p t m", m=P)).then_inc(sg["w_in"], 16)
            sp.dma_start(w_out[:, :, :], T["L0_attn_W_out"].rearrange("(t p) m -> p t m", p=P)).then_inc(sg["w_in"], 16)
            sp.dma_start(A[:, :, :], T["L0_attn_A_log"].rearrange("(t p) n -> p t n", p=P)).then_inc(sg["w_in"], 16)
            sp.dma_start(sel[:, :, :], T["mamba_sel"]).then_inc(sg["w_in"], 16)
            with nc.allow_non_contiguous_dma("biases"):
                sp.dma_start(b_in[:, :], T["L0_attn_b_in"].rearrange("(t p) -> p t", p=P)).then_inc(sg["w_in"], 16)
                sp.dma_start(kern[:, :, :], T["L0_kern"]).then_inc(sg["w_in"], 16)
                sp.dma_start(cols[:, :, :], T["L0_cols"]).then_inc(sg["w_in"], 16)
                sp.dma_start(b_out[:, :], T["L0_attn_b_out"].rearrange("(p a) -> p a", a=1)).then_inc(sg["w_in"], 16)
                sp.dma_start(b_r[:, :], T["L0_attn_b_xp"][0:R].rearrange("(p a) -> p a", a=1)).then_inc(sg["w_in"], 16)
                sp.dma_start(b_n[:, :], T["L0_attn_b_xp"][R:R + 2 * N].rearrange("(p a) -> p a", a=1)).then_inc(sg["w_in"], 16)

        @block.gpsimd
        def _(pool):
            pool.memset(one[:, :], 1.0).then_inc(sg["const"], 1)
            pool.memset(xpad[:, :, :], 0.0).then_inc(sg["const"], 1)
            pool.memset(decay[:, :, :, :, :], 0.0).then_inc(sg["const"], 1)

        def run(eng, group, phase, back, finish):
            def item(n, j, more=True):
                for g in range(G):
                    group(n, j, g)
                    if g == 0 and not (isinstance(n, int) and n == 0):
                        back(n - 1, 1 - j)
                    if more:
                        phase(n + 1, 1 - j, g)

            for g in range(G):
                phase(0, 0, g)
            pairs(eng, B - 2, item)
            item(B - 2, 0)
            item(B - 1, 1, more=False)
            back(B - 1, 1)
            finish()

        @block.tensor
        def _(pe):
            ln.pe(pe)
            pe.wait_ge(sg["ln_log"], B // 2)
            pe.wait_ge(sg["h"], B // 2)
            pe.wait_ge(sg["w_in"], 16 * LOADS)

            def phase(n, j, g):
                if g == 0:
                    hb = ln.h[:, bass.ds(n, 1), :].rearrange("p b s -> p (b s)")
                    wait(pe, sg["relu"], n)
                    wait(pe, sg["soft_abs"], n)
                    for t in range(2):
                        last = pe.matmul(ps_a[:, t, :], w_in[:, t, :], hb, start=True, stop=True)
                    last.then_inc(sg["x_proj"], 1)
                    wait(pe, sg["z"], n)
                    for t in range(2):
                        last = pe.matmul(ps_z[:, t, :], w_in[:, 2 + t, :], hb, start=True, stop=True)
                    last.then_inc(sg["z_proj"], 1)
                if g == 4:
                    pe.wait_ge(sg["gated"], n + 1)
                    wait(pe, sg["biased"], n - 1)
                    for t in range(CT):
                        pe.matmul(ps_c[0:R, 0, :], w_xp[:, t, 0:R], cz[:, j, t, :], start=(t == 0), stop=(t == CT - 1))
                    for t in range(CT):
                        last = pe.matmul(ps_c[0:2 * N, 1, :], w_xp[:, t, R:R + 2 * N], cz[:, j, t, :], start=(t == 0), stop=(t == CT - 1))
                    last.then_inc(sg["dtbc"], 1)
                if g == 5:
                    pe.wait_ge(sg["dti"], n + 1)
                    for t in range(CT):
                        last = pe.matmul(ps_a[:, t, :], w_dt[:, t, :], dti[:, :], start=True, stop=True)
                    last.then_inc(sg["dt_proj"], 1)

            def group(n, j, g):
                pe.wait_ge(sg["dti"], n + 1)
                wait(pe, sg["drive"], G * n + g - 1)
                for k in range(2):
                    last = pe.matmul(ps_b[:, g % 2, 0, k, :], sel[:, 2 * g + k, :], bc[:, j, :], start=True, stop=True)
                last.then_inc(sg["b_spread"], 1)
                wait(pe, sg["read"], G * n + g - 1)
                for k in range(2):
                    last = pe.matmul(ps_n[:, g % 2, 0, k, :], sel[:, N + 2 * g + k, :], bc[:, j, :], start=True, stop=True)
                last.then_inc(sg["c_spread"], 1)
                if g > 0:
                    summed(n, j, g - 1)
                elif not (isinstance(n, int) and n == 0):
                    summed(n - 1, 1 - j, G - 1)

            def summed(n, j, g):
                pe.wait_ge(sg["read"], G * n + g + 1)
                if g == 0:
                    wait(pe, sg["y"], n)
                for k in range(2):
                    last = pe.matmul(ps_y[:, :], core.ident[:, :], read[:, g % 2, :, k, :], start=(g == 0 and k == 0),
                                     stop=(g == G - 1 and k == 1))
                last.then_inc(sg["summed"], 1)

            def back(n, j):
                if isinstance(n, int) and n == B - 1:
                    summed(n, j, G - 1)
                pe.wait_ge(sg["y_gated"], n + 1)
                wait(pe, sg["dti"], n + 2 if not (isinstance(n, int) and n == B - 1) else 0)
                for t in range(CT):
                    last = pe.matmul(ps_c[:, 0, :], w_out[:, t, :], y[:, j, t, :], start=(t == 0), stop=(t == CT - 1))
                last.then_inc(sg["out"], 1)

            run(pe, group, phase, back, lambda: None)

        @block.scalar
        def _(act):
            ln.act(act)
            act.wait_ge(sg["w_in"], 16 * LOADS)
            act.wait_ge(sg["const"], 3)
            nc.scalar.activation(A[:, :, :], A[:, :, :], ACT.Exp).then_inc(sg["A_exp"], 1)
            act.wait_ge(sg["A"], 1)

            def phase(n, j, g):
                if g == 0:
                    act.wait_ge(sg["x_proj"], n + 1)
                    wait(act, sg["conv"], n)
                    for t in range(CT):
                        last = nc.scalar.activation(xpad[:, t, TAPS - 1:], ps_a[:, t, :], ACT.Identity, bias=b_in[:, t:t + 1])
                    last.then_inc(sg["x"], 1)
                    act.wait_ge(sg["z_proj"], n + 1)
                    wait(act, sg["y_gated"], n - 1)
                    for t in range(CT):
                        last = nc.scalar.activation(cz[:, j, 2 + t, :], ps_z[:, t, :], ACT.Identity, bias=b_in[:, 2 + t:3 + t])
                    last.then_inc(sg["z"], 1)
                if g == 2:
                    act.wait_ge(sg["conv"], n + 1)
                    act.wait_ge(sg["z"], n + 1)
                    wait(act, sg["gated"], n)
                    nc.scalar.activation(sg4[:, :, :], cz[:, j, :, :], ACT.Exp, scale=-1.0).then_inc(sg["silu_exp"], 1)
                if g == 4:
                    act.wait_ge(sg["dtbc"], n + 1)
                    wait(act, sg["b_spread"], G * (n - 1))
                    wait(act, sg["c_spread"], G * (n - 1))
                    nc.scalar.activation(bc[:, j, :], ps_c[0:2 * N, 1, :], ACT.Identity, bias=b_n[:, 0:1])
                    nc.scalar.activation(dti[:, :], ps_c[0:R, 0, :], ACT.Identity, bias=b_r[:, 0:1]).then_inc(sg["dti"], 1)
                if g == 5:
                    act.wait_ge(sg["dt_proj"], n + 1)
                    wait(act, sg["dt"], n)
                    for t in range(CT):
                        last = nc.scalar.activation(soft[:, t, :], ps_a[:, t, :], ACT.Abs, bias=cols[:, 1, t:t + 1])
                    last.then_inc(sg["soft_abs"], 1)
                    act.wait_ge(sg["soft_abs"], n + 1)
                    nc.scalar.activation(soft[:, :, :], soft[:, :, :], ACT.Exp, scale=-1.0).then_inc(sg["soft_exp"], 1)
                    act.wait_ge(sg["soft_exp"], n + 1)
                    nc.scalar.activation(soft[:, :, :], soft[:, :, :], ACT.Ln, bias=one[:, 0:1]).then_inc(sg["soft_log"], 1)

            def group(n, j, g):
                act.wait_ge(sg["dt"], n + 1)
                wait(act, sg["scanned"], G * n + g - 1)
                for t in range(CT):
                    for k in range(2):
                        last = nc.scalar.activation(decay[:, g % 2, t, k, 1:], dt[:, j, t, 1:], ACT.Exp,
                                                    scale=A[:, t, 2 * g + k:2 * g + k + 1])
                last.then_inc(sg["decay"], 1)

            def back(n, j):
                act.wait_ge(sg["out"], n + 1)
                wait(act, sg["added"], n - 1)
                nc.scalar.activation(tmp[:, j, :], ps_c[:, 0, :], ACT.Identity, bias=b_out[:, 0:1]).then_inc(sg["biased"], 1)

            run(act, group, phase, back, lambda: None)

        @block.vector
        def _(dve):
            ln.dve(dve)
            dve.wait_ge(sg["w_in"], 16 * LOADS)
            dve.wait_ge(sg["A_exp"], 1)
            nc.vector.tensor_scalar(A[:, :, :], A[:, :, :], -1.0, None, ALU.mult).then_inc(sg["A"], 1)

            def phase(n, j, g):
                if g == 1:
                    dve.wait_ge(sg["x"], n + 1)
                    wait(dve, sg["u"], n - 1)
                    for k in range(TAPS):
                        for t in range(CT):
                            if k == 0:
                                last = nc.vector.tensor_scalar(cz[:, j, t, :], xpad[:, t, 0:S], kern[:, 0, t:t + 1], cols[:, 0, t:t + 1],
                                                               ALU.mult, ALU.add)
                            else:
                                last = nc.vector.scalar_tensor_tensor(out=cz[:, j, t, :], in0=xpad[:, t, k:k + S], scalar=kern[:, k, t:t + 1],
                                                                      in1=cz[:, j, t, :], op0=ALU.mult, op1=ALU.add)
                        if k < TAPS - 1:
                            last.then_inc(sg["tap"], 1)
                            dve.wait_ge(sg["tap"], (TAPS - 1) * n + k + 1)
                    last.then_inc(sg["conv"], 1)
                if g == 3:
                    dve.wait_ge(sg["silu_exp"], n + 1)
                    nc.vector.tensor_scalar(sg4[:, :, :], sg4[:, :, :], 1.0, None, ALU.add).then_inc(sg["silu_den"], 1)
                    dve.wait_ge(sg["silu_den"], 2 * n + 1)
                    nc.vector.reciprocal(sg4[:, :, :], sg4[:, :, :]).then_inc(sg["silu_den"], 1)
                    dve.wait_ge(sg["silu_den"], 2 * n + 2)
                    nc.vector.tensor_tensor(cz[:, j, :, :].rearrange(flat), cz[:, j, :, :].rearrange(flat),
                                            sg4[:, :, :].rearrange(flat), ALU.mult).then_inc(sg["gated"], 1)
                if g == 6:
                    dve.wait_ge(sg["soft_abs"], n + 1)
                    wait(dve, sg["decay"], G * (n - 1))
                    for t in range(CT):
                        last = nc.vector.tensor_scalar(dt[:, j, t, :], ps_a[:, t, :], cols[:, 1, t:t + 1], 0.0, ALU.add, ALU.max)
                    last.then_inc(sg["relu"], 1)
                    dve.wait_ge(sg["relu"], n + 1)
                    dve.wait_ge(sg["soft_log"], n + 1)
                    nc.vector.tensor_tensor(dt[:, j, :, :].rearrange(flat), dt[:, j, :, :].rearrange(flat), soft[:, :, :].rearrange(flat),
                                            ALU.add).then_inc(sg["dt"], 1)
                    dve.wait_ge(sg["dt"], n + 1)
                    nc.vector.tensor_tensor(u[:, j, :, 0, :], dt[:, j, :, :], cz[:, j, 0:CT, :], ALU.mult).then_inc(sg["u"], 1)

            def group(n, j, g):
                dve.wait_ge(sg["b_spread"], G * n + g + 1)
                dve.wait_ge(sg["u"], n + 1)
                nc.vector.tensor_tensor(drive[:, g % 2, :, :, :], u[:, j, :, :, :].to_broadcast([P, CT, 2, S]),
                                        ps_b[:, g % 2, :, :, :].to_broadcast([P, CT, 2, S]), ALU.mult).then_inc(sg["drive"], 1)
                dve.wait_ge(sg["drive"], G * n + g + 1)
                dve.wait_ge(sg["decay"], G * n + g + 1)
                nc.vector.tensor_tensor_scan(state[:, :, :, :].rearrange("p a b s -> p (a b s)"),
                                             decay[:, g % 2, :, :, :].rearrange("p a b s -> p (a b s)"),
                                             drive[:, g % 2, :, :, :].rearrange("p a b s -> p (a b s)"), 0.0,
                                             ALU.mult, ALU.add).then_inc(sg["scanned"], 1)
                dve.wait_ge(sg["scanned"], G * n + g + 1)
                dve.wait_ge(sg["c_spread"], G * n + g + 1)
                wait(dve, sg["summed"], G * n + g - 1)
                nc.vector.tensor_tensor(read[:, g % 2, :, :, :], state[:, :, :, :],
                                        ps_n[:, g % 2, :, :, :].to_broadcast([P, CT, 2, S]), ALU.mult).then_inc(sg["read"], 1)

            def back(n, j):
                dve.wait_ge(sg["summed"], G * (n + 1))
                wait(dve, sg["out"], n - 1)
                for t in range(CT):
                    last = nc.vector.scalar_tensor_tensor(out=y[:, j, t, :], in0=cz[:, j, t, :], scalar=cols[:, 2, t:t + 1],
                                                          in1=ps_y[:, t * S:(t + 1) * S], op0=ALU.mult, op1=ALU.add)
                last.then_inc(sg["y"], 1)
                dve.wait_ge(sg["y"], n + 1)
                nc.vector.tensor_tensor(y[:, j, :, :].rearrange(flat), y[:, j, :, :].rearrange(flat),
                                        cz[:, j, 2:4, :].rearrange(flat), ALU.mult).then_inc(sg["y_gated"], 1)
                if isinstance(n, int) and n == B - 1:
                    residual(n - 1, 1 - j)
                    residual(n, j)
                elif not (isinstance(n, int) and n == 0):
                    residual(n - 1, 1 - j)

            def residual(n, j):
                dve.wait_ge(sg["biased"], n + 1)
                add_residual(core, sg, dve, n, tmp[:, j, :], n, 0, GATE_A).then_inc(sg["added"], 1)

            run(dve, group, phase, back, lambda: None)


def stage_moe(core, T):
    nc, B, S = core.nc, core.B, core.S
    E = T["L2_ffn_router_w"].shape[1]
    PAIRS = E // 2 + 1
    W = 2 * S
    TT = W // P
    with ExitStack() as ctx:
        sg = Signals(nc, ctx, "mo")

        def sb(name, shape, dt=F32):
            return ctx.enter_context(nc.sbuf_tensor("mo_" + name, shape, dt))

        def psum(name, shape, dt=F32):
            return ctx.enter_context(nc.psum_tensor("mo_" + name, shape, dt))

        ln = AdaNorm(core, ctx, sg, 2, SHIFT_B, SCALE_B)
        wr = sb("wr", [P, E])
        br = sb("br", [P, 1, E])
        rank = sb("rank", [P, 1, E])
        w13 = sb("w13", [P, 2, PAIRS, P])
        w2 = sb("w2", [P, PAIRS, P])
        spread = sb("spread", [E, PAIRS - 1, P])
        gatesT = sb("gatesT", [E, B * S])
        h_fixed = sb("h_fixed", [P, 2, W])
        logit = sb("logit", [P, TT, E])
        rest = sb("rest", [P, TT, E])
        cand = sb("cand", [P, TT, E])
        best = sb("best", [P, 2, TT, E])
        top = sb("top", [P, 2, TT, 1])
        ctop = sb("ctop", [P, TT, 1])
        gate = sb("gate", [P, 2, TT, E])
        gsum = sb("gsum", [P, TT, 1])
        act1 = sb("act1", [P, 2, W])
        hid = sb("hid", [P, 2, W])
        ps_r = psum("ps_r", [P, 2, W])
        ps_g = psum("ps_g", [P, 2, W])
        ps_h = psum("ps_h", [P, 2, 2, W])
        ln.ps_mean, ln.ps_var = ps_r, ps_g
        items = B // 2
        block = ctx.enter_context(nc.Block())

        @block.sync
        def _(sp):
            sp.dma_start(wr[:, :], T["L2_ffn_router_w"]).then_inc(sg["w_in"], 16)
            sp.dma_start(br[:, 0, :], T["L2_ffn_router_b"].rearrange("(a n) -> a n", a=1).to_broadcast([P, E])).then_inc(sg["w_in"], 16)
            sp.dma_start(rank[:, 0, :], T["moe_rank"]).then_inc(sg["w_in"], 16)
            sp.dma_start(w13[:, :, :, :], T["L2_w13"]).then_inc(sg["w_in"], 16)
            sp.dma_start(w2[:, :, :], T["L2_w2"]).then_inc(sg["w_in"], 16)
            sp.dma_start(spread[:, :, :], T["moe_spread"]).then_inc(sg["w_in"], 16)

        @block.gpsimd
        def _(pool):
            def item(n, j):
                pool.wait_ge(sg["h"], items)
                wait(pool, sg["logits"], n - 1)
                pool.tensor_copy(h_fixed[:, j, :], ln.h[:, bass.ds(2 * n, 2), :].rearrange("p b s -> p (b s)")).then_inc(sg["h_fixed"], 1)

            pairs(pool, items, item)

        @block.tensor
        def _(pe):
            ln.pe(pe)
            pe.wait_ge(sg["ln_log"], items)
            pe.wait_ge(sg["w_in"], 16 * 6)

            def route(n, j):
                pe.wait_ge(sg["h_fixed"], n + 1)
                wait(pe, sg["logit_read"], n)
                for t in range(TT):
                    last = pe.matmul(ps_r[:, 0, t * E:(t + 1) * E], h_fixed[:, j, t * P:(t + 1) * P], wr[:, :], start=True, stop=True)
                last.then_inc(sg["logits"], 1)
                pe.wait_ge(sg["gate"], n + 1)
                wait(pe, sg["gateT"], n)
                for t in range(TT):
                    last = pe.transpose(ps_r[0:E, 1, t * P:(t + 1) * P], gate[:, j, t, :], core.ident[:, :])
                last.then_inc(sg["gate_turned"], 1)

            pairs(pe, items, route)
            pe.wait_ge(sg["gateT"], items)

            def item(n, j):
                h2 = ln.h[:, bass.ds(2 * n, 2), :].rearrange("p b s -> p (b s)")

                def up(e):
                    wait(pe, sg["hid"], PAIRS * n + e - 1)
                    for k in range(2):
                        if k == 1:
                            wait(pe, sg["hid"], PAIRS * n + e)
                        last = pe.matmul(ps_h[:, e % 2, k, :], w13[:, k, e, :], h2, start=True, stop=True)
                    if e < PAIRS - 1:
                        last = pe.matmul(ps_g[:, 0, :], spread[:, e, :], gatesT[:, bass.ds(W * n, W)], start=True, stop=True)
                    last.then_inc(sg["up"], 1)

                def down(e):
                    pe.wait_ge(sg["hid"], PAIRS * n + e + 1)
                    if e == 0:
                        wait(pe, sg["added"], n)
                    last = pe.matmul(ps_g[:, 1, :], w2[:, e, :], hid[:, e % 2, :], start=(e == 0), stop=(e == PAIRS - 1))
                    last.then_inc(sg["down"], 1)

                up(0)
                for e in range(1, PAIRS):
                    up(e)
                    down(e - 1)
                down(PAIRS - 1)

            items_loop(pe, items, item)

        @block.scalar
        def _(act):
            ln.act(act)

            def route(n, j):
                act.wait_ge(sg["shifted"], n + 1)
                nc.scalar.activation(gate[:, j, :, :], gate[:, j, :, :], ACT.Exp).then_inc(sg["route_exp"], 1)
                act.wait_ge(sg["gate_turned"], n + 1)
                act.copy(gatesT[:, bass.ds(W * n, W)], ps_r[0:E, 1, :]).then_inc(sg["gateT"], 1)

            pairs(act, items, route)

            def item(n, j):
                for e in range(PAIRS):
                    act.wait_ge(sg["up"], PAIRS * n + e + 1)
                    wait(act, sg["hid"], PAIRS * n + e - 1)
                    nc.scalar.activation(act1[:, e % 2, :], ps_h[:, e % 2, 0, :], ACT.Silu).then_inc(sg["silu"], 1)

            items_loop(act, items, item)

        @block.vector
        def _(dve):
            ln.dve(dve)
            dve.wait_ge(sg["w_in"], 16 * 6)

            def route(n, j):
                steps = 10

                def done(ins, k):
                    ins.then_inc(sg["route"], 1)
                    dve.wait_ge(sg["route"], steps * n + k)

                dve.wait_ge(sg["logits"], n + 1)
                ps = ps_r[:, 0, 0:TT * E].rearrange("p (t e) -> p t e", e=E)
                nc.vector.tensor_tensor(logit[:, :, :], ps, br[:, :, :].to_broadcast([P, TT, E]), ALU.add).then_inc(sg["logit_read"], 1)
                dve.wait_ge(sg["logit_read"], n + 1)
                for k, src in enumerate((logit, rest)):
                    done(nc.vector.tensor_reduce(top[:, k, :, 0], src[:, :, :], AX.X, ALU.max), 4 * k + 1 + k)
                    done(nc.vector.tensor_tensor(cand[:, :, :], src[:, :, :], top[:, k, :, :].to_broadcast([P, TT, E]), ALU.is_equal), 4 * k + 2 + k)
                    done(nc.vector.tensor_tensor(cand[:, :, :], cand[:, :, :], rank[:, :, :].to_broadcast([P, TT, E]), ALU.mult), 4 * k + 3 + k)
                    done(nc.vector.tensor_reduce(ctop[:, :, 0], cand[:, :, :], AX.X, ALU.max), 4 * k + 4 + k)
                    if k == 0:
                        nc.vector.tensor_tensor(best[:, 0, :, :], cand[:, :, :], ctop[:, :, :].to_broadcast([P, TT, E]), ALU.is_equal).then_inc(sg["best"], 1)
                        dve.wait_ge(sg["best"], 2 * n + 1)
                        done(nc.vector.scalar_tensor_tensor(out=rest[:, :, :].rearrange("p t e -> p (t e)"),
                                                            in0=best[:, 0, :, :].rearrange("p t e -> p (t e)"), scalar=-1e30,
                                                            in1=logit[:, :, :].rearrange("p t e -> p (t e)"), op0=ALU.mult,
                                                            op1=ALU.add), 5)
                    else:
                        done(nc.vector.tensor_tensor(best[:, 1, :, :], cand[:, :, :], ctop[:, :, :].to_broadcast([P, TT, E]), ALU.is_equal), 10)
                nc.vector.tensor_tensor(best[:, 0, :, :], best[:, 0, :, :], best[:, 1, :, :], ALU.add).then_inc(sg["best"], 1)
                wait(dve, sg["gate_turned"], n - 1)
                nc.vector.tensor_tensor(gate[:, j, :, :], logit[:, :, :], top[:, 0, :, :].to_broadcast([P, TT, E]), ALU.subtract).then_inc(sg["shifted"], 1)
                dve.wait_ge(sg["best"], 2 * n + 2)
                dve.wait_ge(sg["route_exp"], n + 1)
                nc.vector.tensor_tensor(gate[:, j, :, :], gate[:, j, :, :], best[:, 0, :, :], ALU.mult).then_inc(sg["gated"], 1)
                dve.wait_ge(sg["gated"], 3 * n + 1)
                nc.vector.tensor_reduce(gsum[:, :, 0], gate[:, j, :, :], AX.X, ALU.add).then_inc(sg["gated"], 1)
                dve.wait_ge(sg["gated"], 3 * n + 2)
                nc.vector.reciprocal(gsum[:, :, :], gsum[:, :, :]).then_inc(sg["gated"], 1)
                dve.wait_ge(sg["gated"], 3 * n + 3)
                nc.vector.tensor_tensor(gate[:, j, :, :], gate[:, j, :, :], gsum[:, :, :].to_broadcast([P, TT, E]), ALU.mult).then_inc(sg["gate"], 1)

            pairs(dve, items, route)

            def item(n, j):
                for e in range(PAIRS):
                    dve.wait_ge(sg["silu"], PAIRS * n + e + 1)
                    wait(dve, sg["down"], PAIRS * n + e - 1)
                    up = nc.vector.tensor_tensor(hid[:, e % 2, :], act1[:, e % 2, :], ps_h[:, e % 2, 1, :], ALU.mult)
                    if e < PAIRS - 1:
                        up.then_inc(sg["ungated"], 1)
                        dve.wait_ge(sg["ungated"], (PAIRS - 1) * n + e + 1)
                        up = nc.vector.tensor_tensor(hid[:, e % 2, :], hid[:, e % 2, :], ps_g[:, 0, :], ALU.mult)
                    up.then_inc(sg["hid"], 1)
                dve.wait_ge(sg["down"], PAIRS * (n + 1))
                for k in range(2):
                    last = add_residual(core, sg, dve, n, ps_g[:, 1, k * S:(k + 1) * S], 2 * n + k, 2, GATE_B)
                last.then_inc(sg["added"], 1)

            items_loop(dve, items, item)


STAGES = (stage_mamba, stage_fp4_ffn, stage_diff_attention, stage_local_transformer,
          stage_gqa_attention, stage_moe, stage_causal_attention, stage_binary_ffn)


def build_program(nc, T, out):
    with ExitStack() as ctx:
        core = open_core(nc, ctx, T["L0_attn_x"])
        stage_load(core, T)
        for stage in STAGES:
            stage(core, T)
        stage_store(core, out)


def kernel(**inputs):
    import concourse.bacc as bacc
    from concourse.bass_utils import run_bass_kernel_spmd

    nc = bacc.Bacc("TRN2", target_bir_lowering=False, num_devices=1)
    arrays, T = {}, {}
    given = {name: np.ascontiguousarray(a) for name, a in inputs.items()}
    for name, a in {**given, **shape_constants(given)}.items():
        arrays[f"in_{name}"] = a
        T[name] = nc.dram_tensor(f"in_{name}", a.shape, mybir.dt.from_np(a.dtype), kind="ExternalInput").ap()
    shape = given["L0_attn_x"].shape
    out = nc.dram_tensor("out", shape, F32, kind="ExternalOutput").ap()
    build_program(nc, T, out)
    r = run_bass_kernel_spmd(nc, [arrays], core_ids=[0])
    return r.results[0]["out"]
```
